# Optimizing a Trainium2 kernel written in Bass

```python
import numpy as np
import jax
import jax.numpy as jnp

def _softmax(x, axis=-1):
    return jax.nn.softmax(x, axis=axis)

def _gelu(x):
    return jax.nn.gelu(x, approximate=True)

def _silu(x):
    return jax.nn.silu(x)

def _sigmoid(x):
    return jax.nn.sigmoid(x)

def _layernorm(x, axis=-1, eps=1e-05):
    m = jnp.mean(x, axis=axis, keepdims=True)
    v = jnp.var(x, axis=axis, keepdims=True)
    return (x - m) / jnp.sqrt(v + eps)

def _scatter_add(tgt, idx, src, axis=0):
    return tgt.at[idx].add(src)

def _segment_sum(src, seg, n):
    return jax.ops.segment_sum(src, seg, n)
kernel_name = 'mk_cond_resid_d4_seqx_r8_aa1aa4'

def setup_inputs(seed: int=0):
    np.random.seed(seed)
    _w = jnp.asarray

    def _rec_inputs():
        import jax
        import jax.numpy as jnp
        _rk = jax.random.key(seed)
        x = -7.109e-05 + 0.9999 * jax.random.normal(jax.random.fold_in(_rk, 1), (32, 128, 128), jnp.float32)
        _lenS = 128 - jax.random.randint(jax.random.fold_in(_rk, 7), (32,), 0, max(1, 128 // 4) + 1, jnp.int32)
        _lenS2 = 128 - jax.random.randint(jax.random.fold_in(_rk, 8), (32,), 0, max(1, 128 // 4) + 1, jnp.int32)
        itok_B_0_3 = jax.random.randint(jax.random.fold_in(_rk, 11), (32,), 0, 4, jnp.int32)
        fside_BxSxS_0 = 4.13588e-05 + 0.999923 * jax.random.normal(jax.random.fold_in(_rk, 12), (32, 128, 128), jnp.float32)
        itok_B_18_1004 = jax.random.randint(jax.random.fold_in(_rk, 13), (32,), 18, 1005, jnp.int32)
        itok_B_0_2 = jax.random.randint(jax.random.fold_in(_rk, 14), (32,), 0, 3, jnp.int32)
        return (x, itok_B_0_3, fside_BxSxS_0, itok_B_18_1004, itok_B_0_2)
    x, itok_B_0_3, fside_BxSxS_0, itok_B_18_1004, itok_B_0_2 = _rec_inputs()

    def _L0_cond_setup():
        import jax, jax.numpy as jnp
        import numpy as np
        D = 128
        RANK = 16
        ALPHA = 16.0
        SCALING = ALPHA / RANK
        N_LANG = 4
        B, S = (32, 256)
        key = jax.random.key(seed)
        k1, k2, k3, k4, k5 = jax.random.split(key, 5)
        x = jax.random.normal(k1, (B, S, D), dtype=jnp.float32)
        language_ids = jax.random.randint(k2, (B,), 0, N_LANG, dtype=jnp.int32)
        lora_A = jax.random.normal(k3, (N_LANG, RANK, D), dtype=jnp.float32) * 0.02
        lora_B = jax.random.normal(k4, (N_LANG, D, RANK), dtype=jnp.float32) * 0.02
        lang_embed = jax.random.normal(k5, (N_LANG, D), dtype=jnp.float32) * 0.02
        return {'x': x, 'language_ids': language_ids, 'lora_A': lora_A, 'lora_B': lora_B, 'lang_embed': lang_embed}
    _L0_cond_all = _L0_cond_setup()
    _L0_cond_in = {k: v for k, v in _L0_cond_all.items() if k in ('lora_A', 'lora_B', 'lang_embed')}
    del _L0_cond_all

    def _L1_cond_setup():
        import jax, jax.numpy as jnp
        import numpy as np
        B, L1, L2, DIN, DOUT, H = (8, 128, 128, 128, 128, 16)
        DH = DOUT // H
        SCALE = 1.0 / np.sqrt(DH).astype(np.float32)
        key = jax.random.key(seed)
        ks = jax.random.split(key, 13)
        s = 0.02
        return {'seq1': jax.random.normal(ks[0], (B, L1, DIN), jnp.float32), 'seq2': jax.random.normal(ks[1], (B, L2, DIN), jnp.float32), 'seq_len1': jax.random.randint(ks[2], (B,), 1, L1 + 1, jnp.int32), 'Wq': jax.random.normal(ks[3], (DIN, DOUT), jnp.float32) * s, 'bq': jnp.zeros((DOUT,), jnp.float32), 'Wk': jax.random.normal(ks[4], (DIN, DOUT), jnp.float32) * s, 'bk': jnp.zeros((DOUT,), jnp.float32), 'Wv': jax.random.normal(ks[5], (DIN, DOUT), jnp.float32) * s, 'bv': jnp.zeros((DOUT,), jnp.float32), 'Wo': jax.random.normal(ks[6], (DOUT, DOUT), jnp.float32) * s, 'bo': jnp.zeros((DOUT,), jnp.float32), 'b_prev': jax.random.normal(ks[7], (1, 1, DIN), jnp.float32) * s, 'b_self': jax.random.normal(ks[8], (1, 1, DIN), jnp.float32) * s}
    _L1_cond_all = _L1_cond_setup()
    _L1_cond_in = {k: v for k, v in _L1_cond_all.items() if k in ('Wq', 'bq', 'Wk', 'bk', 'Wv', 'bv', 'Wo', 'bo', 'b_prev', 'b_self')}
    del _L1_cond_all

    def _L2_cond_setup():
        import jax, jax.numpy as jnp
        import numpy as np
        B, S, D, F, E = (8, 256, 128, 512, 5)

        def _dense(x, wi_, wo_):
            return jax.nn.relu(x @ wi_) @ wo_
        key = jax.random.key(seed)
        ks = jax.random.split(key, 9)
        sc = 0.02
        return {'hidden_states': jax.random.normal(ks[0], (B, S, D), jnp.float32), 'type_label': jax.random.randint(ks[1], (B,), 0, E, jnp.int32), 'wi': jax.random.normal(ks[2], (E, D, F), jnp.float32) * sc, 'wo': jax.random.normal(ks[3], (E, F, D), jnp.float32) * sc, 'swi': jax.random.normal(ks[4], (2, D, F), jnp.float32) * sc, 'swo': jax.random.normal(ks[5], (2, F, D), jnp.float32) * sc, 'g1': jax.random.normal(ks[6], (3 * D, D), jnp.float32) * sc, 'g2': jax.random.normal(ks[7], (D, 3), jnp.float32) * sc}
    _L2_cond_all = _L2_cond_setup()
    _L2_cond_in = {k: v for k, v in _L2_cond_all.items() if k in ('wi', 'wo', 'swi', 'swo', 'g1', 'g2')}
    del _L2_cond_all

    def _L3_cond_setup():
        import jax, jax.numpy as jnp
        import numpy as np
        B, S, D, F, E = (8, 128, 128, 512, 4)

        def _dense(x, wi, wo):
            return jax.nn.relu(x @ wi) @ wo
        key = jax.random.key(seed)
        ks = jax.random.split(key, 10)
        scale = 0.02
        return {'hidden_states': jax.random.normal(ks[0], (B, S, D), jnp.float32), 'type_idx': jax.random.randint(ks[1], (B,), 0, 3, jnp.int32), 'expert_wi': jax.random.normal(ks[2], (E, D, F), jnp.float32) * scale, 'expert_wo': jax.random.normal(ks[3], (E, F, D), jnp.float32) * scale, 'share_wi': jax.random.normal(ks[4], (3, D, F), jnp.float32) * scale, 'share_wo': jax.random.normal(ks[5], (3, F, D), jnp.float32) * scale, 'gate_vecs': jnp.array([[0.22, 0.22, 0.2, 0.2], [0.2, 0.22, 0.22, 0.2], [0.2, 0.2, 0.22, 0.22]], jnp.float32), 'gate_w1': jax.random.normal(ks[6], (4 * D, D), jnp.float32) * scale, 'gate_w2': jax.random.normal(ks[7], (D, 4), jnp.float32) * scale}
    _L3_cond_all = _L3_cond_setup()
    _L3_cond_in = {k: v for k, v in _L3_cond_all.items() if k in ('expert_wi', 'expert_wo', 'share_wi', 'share_wo', 'gate_vecs', 'gate_w1', 'gate_w2')}
    del _L3_cond_all
    return {'x': x, 'itok_B_0_3': itok_B_0_3, 'fside_BxSxS_0': fside_BxSxS_0, 'itok_B_18_1004': itok_B_18_1004, 'itok_B_0_2': itok_B_0_2, 'L0_cond_lora_A': _L0_cond_in['lora_A'], 'L0_cond_lora_B': _L0_cond_in['lora_B'], 'L0_cond_lang_embed': _L0_cond_in['lang_embed'], 'L1_cond_Wq': _L1_cond_in['Wq'], 'L1_cond_bq': _L1_cond_in['bq'], 'L1_cond_Wk': _L1_cond_in['Wk'], 'L1_cond_bk': _L1_cond_in['bk'], 'L1_cond_Wv': _L1_cond_in['Wv'], 'L1_cond_bv': _L1_cond_in['bv'], 'L1_cond_Wo': _L1_cond_in['Wo'], 'L1_cond_bo': _L1_cond_in['bo'], 'L1_cond_b_prev': _L1_cond_in['b_prev'], 'L1_cond_b_self': _L1_cond_in['b_self'], 'L2_cond_wi': _L2_cond_in['wi'], 'L2_cond_wo': _L2_cond_in['wo'], 'L2_cond_swi': _L2_cond_in['swi'], 'L2_cond_swo': _L2_cond_in['swo'], 'L2_cond_g1': _L2_cond_in['g1'], 'L2_cond_g2': _L2_cond_in['g2'], 'L3_cond_expert_wi': _L3_cond_in['expert_wi'], 'L3_cond_expert_wo': _L3_cond_in['expert_wo'], 'L3_cond_share_wi': _L3_cond_in['share_wi'], 'L3_cond_share_wo': _L3_cond_in['share_wo'], 'L3_cond_gate_vecs': _L3_cond_in['gate_vecs'], 'L3_cond_gate_w1': _L3_cond_in['gate_w1'], 'L3_cond_gate_w2': _L3_cond_in['gate_w2']}

def reference(x, itok_B_0_3, fside_BxSxS_0, itok_B_18_1004, itok_B_0_2, L0_cond_lora_A, L0_cond_lora_B, L0_cond_lang_embed, L1_cond_Wq, L1_cond_bq, L1_cond_Wk, L1_cond_bk, L1_cond_Wv, L1_cond_bv, L1_cond_Wo, L1_cond_bo, L1_cond_b_prev, L1_cond_b_self, L2_cond_wi, L2_cond_wo, L2_cond_swi, L2_cond_swo, L2_cond_g1, L2_cond_g2, L3_cond_expert_wi, L3_cond_expert_wo, L3_cond_share_wi, L3_cond_share_wo, L3_cond_gate_vecs, L3_cond_gate_w1, L3_cond_gate_w2):
    import jax
    import jax.numpy as jnp

    def _L0_cond_ref(x, language_ids, lora_A, lora_B, lang_embed):
        import jax, jax.numpy as jnp
        import numpy as np
        D = 128
        RANK = 16
        ALPHA = 16.0
        SCALING = ALPHA / RANK
        N_LANG = 4
        B, S = (32, 256)
        A = lora_A[language_ids]
        Bm = lora_B[language_ids]
        emb = lang_embed[language_ids]
        t = jnp.einsum('bsd,brd->bsr', x, A)
        lora_out = jnp.einsum('bsr,bdr->bsd', t, Bm) * SCALING
        return lora_out + emb[:, None, :]

    def _L1_cond_ref(seq1, seq2, seq_len1, Wq, bq, Wk, bk, Wv, bv, Wo, bo, b_prev, b_self):
        import jax, jax.numpy as jnp
        import numpy as np
        B, L1, L2, DIN, DOUT, H = (8, 128, 128, 128, 128, 16)
        DH = DOUT // H
        SCALE = 1.0 / np.sqrt(DH).astype(np.float32)
        b, l1, _ = seq1.shape
        l2 = seq2.shape[1]
        query = seq2 + b_self
        key = jnp.concatenate([seq1 + b_prev, seq2 + b_self], 1)
        value = jnp.concatenate([seq1, seq2], 1)
        q = (query @ Wq + bq).reshape(b, l2, H, DH).transpose(0, 2, 1, 3)
        k = (key @ Wk + bk).reshape(b, l1 + l2, H, DH).transpose(0, 2, 1, 3)
        v = (value @ Wv + bv).reshape(b, l1 + l2, H, DH).transpose(0, 2, 1, 3)
        score_prev = jnp.einsum('bhqd,bhkd->bhqk', q, k[:, :, :l1]) * SCALE
        score_self = (q * k[:, :, l1:]).sum(-1, keepdims=True) * SCALE
        mask = jnp.arange(l1)[None, :] < seq_len1[:, None]
        score_prev = jnp.where(mask[:, None, None, :], score_prev, -jnp.inf)
        score = jnp.concatenate([score_prev, score_self], -1)
        weights = jax.nn.softmax(score, axis=-1)
        attn = jnp.einsum('bhqk,bhkd->bhqd', weights[..., :-1], v[:, :, :l1])
        attn = attn + weights[..., -1:] * v[:, :, l1:]
        attn = attn.transpose(0, 2, 1, 3).reshape(b, l2, H * DH)
        return attn @ Wo + bo

    def _L2_cond_ref(hidden_states, type_label, wi, wo, swi, swo, g1, g2):
        import jax, jax.numpy as jnp
        import numpy as np
        B, S, D, F, E = (8, 256, 128, 512, 5)

        def _dense(x, wi_, wo_):
            return jax.nn.relu(x @ wi_) @ wo_
        x = hidden_states
        s0 = _dense(x, swi[0], swo[0])
        s1 = _dense(x, swi[1], swo[1])
        wi_sel = wi[type_label]
        wo_sel = wo[type_label]
        h = jax.nn.relu(jnp.einsum('bsd,bdf->bsf', x, wi_sel))
        eo = jnp.einsum('bsf,bfd->bsd', h, wo_sel)
        gate_in = jnp.concatenate([eo[:, 0], s0[:, 0], s1[:, 0]], axis=-1)
        w = jax.nn.softmax(jax.nn.relu(gate_in @ g1) @ g2, axis=-1)
        w = w[:, :, None, None]
        return eo * w[:, 0] + s0 * w[:, 1] + s1 * w[:, 2]

    def _L3_cond_ref(hidden_states, type_idx, expert_wi, expert_wo, share_wi, share_wo, gate_vecs, gate_w1, gate_w2):
        import jax, jax.numpy as jnp
        import numpy as np
        B, S, D, F, E = (8, 128, 128, 512, 4)

        def _dense(x, wi, wo):
            return jax.nn.relu(x @ wi) @ wo
        s0 = _dense(hidden_states, share_wi[0], share_wo[0])
        s1 = _dense(hidden_states, share_wi[1], share_wo[1])
        s2 = _dense(hidden_states, share_wi[2], share_wo[2])
        idx_a = type_idx
        idx_b = type_idx + 1
        out_a = jnp.einsum('bsf,bfd->bsd', jax.nn.relu(jnp.einsum('bsd,bdf->bsf', hidden_states, expert_wi[idx_a])), expert_wo[idx_a])
        out_b = jnp.einsum('bsf,bfd->bsd', jax.nn.relu(jnp.einsum('bsd,bdf->bsf', hidden_states, expert_wi[idx_b])), expert_wo[idx_b])
        p = jax.nn.softmax(gate_vecs / 0.1, axis=-1)
        wa = p[type_idx, idx_a][:, None, None]
        wb = p[type_idx, idx_b][:, None, None]
        expert_out = out_a * wa + out_b * wb
        gi = jnp.concatenate([expert_out[:, 0], s0[:, 0], s1[:, 0], s2[:, 0]], axis=-1)
        g = jax.nn.softmax(jax.nn.relu(gi @ gate_w1) @ gate_w2, axis=-1)
        out = expert_out * g[:, 0, None, None] + s0 * g[:, 1, None, None] + s1 * g[:, 2, None, None] + s2 * g[:, 3, None, None]
        return out
    x = x + _L0_cond_ref(x, itok_B_0_3, L0_cond_lora_A, L0_cond_lora_B, L0_cond_lang_embed)
    x = x + _L1_cond_ref(x, fside_BxSxS_0, itok_B_18_1004, L1_cond_Wq, L1_cond_bq, L1_cond_Wk, L1_cond_bk, L1_cond_Wv, L1_cond_bv, L1_cond_Wo, L1_cond_bo, L1_cond_b_prev, L1_cond_b_self)
    x = x + _L2_cond_ref(x, itok_B_0_2, L2_cond_wi, L2_cond_wo, L2_cond_swi, L2_cond_swo, L2_cond_g1, L2_cond_g2)
    x = x + _L3_cond_ref(x, itok_B_0_2, L3_cond_expert_wi, L3_cond_expert_wo, L3_cond_share_wi, L3_cond_share_wo, L3_cond_gate_vecs, L3_cond_gate_w1, L3_cond_gate_w2)
    return x

_drawn_inputs = setup_inputs


def setup_inputs(seed=0):
    import zlib

    import numpy as np

    out = dict(_drawn_inputs(seed))
    spreads = {'L1_cond_bq': (0.0, 0.8),
     'L1_cond_bk': (0.0, 0.8),
     'L1_cond_bv': (0.0, 0.379),
     'L1_cond_bo': (0.0, 0.1)}
    factors = {'fside_BxSxS_0': 8.0,
     'L0_cond_lora_A': 3.119,
     'L0_cond_lora_B': 3.124,
     'L0_cond_lang_embed': 2.878,
     'L1_cond_Wq': 8.0,
     'L1_cond_Wk': 8.0,
     'L1_cond_Wv': 8.0,
     'L1_cond_b_prev': 8.0,
     'L1_cond_b_self': 8.0,
     'L2_cond_wi': 2.854,
     'L2_cond_g1': 8.0,
     'L2_cond_g2': 8.0,
     'L3_cond_expert_wi': 8.0,
     'L3_cond_expert_wo': 8.0,
     'L3_cond_gate_vecs': 8.0,
     'L3_cond_gate_w1': 8.0,
     'L3_cond_gate_w2': 8.0}
    for name, (base, spread) in spreads.items():
        noise = np.random.default_rng([zlib.crc32(name.encode()), seed]).standard_normal(out[name].shape)
        drawn = base * np.exp(spread * noise) if base else spread * noise
        out[name] = jnp.asarray(drawn.astype(out[name].dtype))
    for name, factor in factors.items():
        out[name] = (out[name] * factor).astype(out[name].dtype)
    return out
```

```python
from contextlib import ExitStack

import numpy as np

import concourse.bass as bass
from concourse import mybir

ALU = mybir.AluOpType
ACT = mybir.ActivationFunctionType
AXX = mybir.AxisListType.X
F32 = mybir.dt.float32
F32R = mybir.dt.float32r
I32 = mybir.dt.int32
U8 = mybir.dt.uint8

P = 128
NB = 4
H = 16
DH = P // H
G = 4
J = H // G
FC = 4
LANGS, RANK = 4, 16
LR = LANGS * RANK
TYPES = 3
SCALE = float(np.float32(1.0) / np.sqrt(np.float32(DH)))
RING = 6

OUTS = [(2, "expert", 0), (2, "shared", 0), (2, "shared", 1),
        (3, "shared", 2), (3, "shared", 3), (3, "shared", 4), (3, "expert", 1), (3, "expert", 2)]
UNITS = 4 * len(OUTS)
L3_FIRST = 12
NO = len(OUTS)
EXPERT_UNITS = [4 * o + b for o, (_, kind, _) in enumerate(OUTS) if kind == "expert" for b in range(NB)]
SHARED_BEFORE = [sum(OUTS[v // 4][1] == "shared" for v in range(u)) for u in range(UNITS + 1)]
NSHARED = SHARED_BEFORE[UNITS]


def make_schedule():
    a = lambda name, k=0: ("a", name, k)
    f = lambda name, k=0: ("f", name, k)
    steps = [a("load")]
    att = {2: [a("lora1")], 4: [a("lora2")], 6: [a("proj")], 7: [a("self")], 8: [a("stack")]}
    for u in range(L3_FIRST):
        steps.append(f("unit", u))
        steps += att.get(u, [])
    steps += [f("l2end")]
    steps += [f("hid", 0), a("S", 0), f("logit", 0), a("S", 1), f("soft", 0), a("S", 2), f("mix2"), a("S", 3)]
    e = 0
    for u in range(L3_FIRST, UNITS):
        steps.append(f("unit", u))
        if u == L3_FIRST + 1:
            steps.append(a("mq"))
        if u >= L3_FIRST + 4:
            if e < NB * G:
                steps.append(a("E", e))
                e += 1
    steps += [a("Eend"), f("l3end"), f("exmix"), a("fin"), f("hid", 1), f("logit", 1), f("soft", 1), a("wo"), f("mix3")]
    assert e == NB * G
    return steps


SCHEDULE = make_schedule()


def cond_resid_kernel(nc, xT, sT, lens, labels, langs, loraA, loraBe, wqkvo, vecs, shared, experts2,
                      experts3, g1, g2r, gw1, gw2r, gate_vecs, consts, out):
    groups = xT.shape[0]
    NSEQ = groups * NB
    E2, E3 = experts2.shape[0], experts3.shape[0]
    NS = shared.shape[1]
    FW = shared.shape[2]
    F = FC * P
    experts = [experts2, experts3, experts3]

    with ExitStack() as ctx:
        def sb(name, shape, dt=F32):
            return ctx.enter_context(nc.sbuf_tensor(name, shape, dt))

        def ps(name, shape):
            return ctx.enter_context(nc.psum_tensor(name, shape, F32))

        def sem(name):
            return ctx.enter_context(nc.semaphore(name))

        bank_a = [ps(f"bank_a{k}", [P, 512]) for k in range(4)]
        bank_h = [ps(f"bank_h{k}", [P, 512]) for k in range(2)]
        bank_o = [ps(f"bank_o{k}", [P, 512]) for k in range(2)]

        ring = sb("ring", [P, RING, FW])
        sh_hi = sb("sh_hi", [P, NS, FW], F32R)
        sh_lo = sb("sh_lo", [P, NS, FW], F32R)
        wraw = sb("wraw", [P, 4, P])
        w_hi = sb("w_hi", [P, 3, P], F32R)
        w_lo = sb("w_lo", [P, 3, P], F32R)
        lora_a = sb("lora_a", [P, LR])
        lora_be = sb("lora_be", [LR + LANGS, P])
        g1_sb = sb("g1_sb", [P, 3, P])
        g2_sb = sb("g2_sb", [P, 3, P])
        gw1_sb = sb("gw1_sb", [P, 4, P])
        gw2_sb = sb("gw2_sb", [P, 4, P])
        vec = sb("vec", [P, 6])
        bias = sb("bias", [P, 4])
        bq_s = sb("bq_s", [P, 1])
        const = sb("const", [P, 3 * P + 3])
        ident = const[:, 0:P]
        head_sum = const[:, P:2 * P]
        key_no = const[:, 2 * P:3 * P]
        part_no = const[:, 3 * P:3 * P + 1]
        lang_no = const[:, 3 * P + 1:3 * P + 2]
        shift_row = const[:, 3 * P + 2:3 * P + 3]

        ints = sb("ints", [P, 3, NSEQ], I32)
        lens_f = sb("lens_f", [P, NSEQ])
        labels_f = sb("labels_f", [P, NSEQ])
        langs_f = sb("langs_f", [P, NSEQ])
        key_mask = sb("key_mask", [P, NSEQ])
        lang_hot = sb("lang_hot", [P, NSEQ])
        gv = sb("gv", [P, TYPES, 4])
        gv_s = sb("gv_s", [P, TYPES])
        wab = sb("wab", [P, 2, NSEQ])
        wab_t = sb("wab_t", [P, NSEQ])

        x1 = sb("x1", [P, NB, P])
        s2 = sb("s2", [P, NB, P])
        x1_hi = sb("x1_hi", [P, NB, P], F32R)
        x1_lo = sb("x1_lo", [P, NB, P], F32R)
        s2_hi = sb("s2_hi", [P, NB, P], F32R)
        s2_lo = sb("s2_lo", [P, NB, P], F32R)
        adapt = sb("adapt", [LR + LANGS, NB, P])
        hot_g = sb("hot_g", [P, NB])
        len_g = sb("len_g", [P, NB])
        mask_g = sb("mask_g", [P, NB])
        wab_g = sb("wab_g", [P, 2, NB])
        pad_key = sb("pad_key", [P, NB, P], U8)
        kf = sb("kf", [P, NB, P])
        k_first = sb("k_first", [P, NB])
        k_self = sb("k_self", [P, NB, P])
        v_self = sb("v_self", [P, NB, P])
        s_self = sb("s_self", [P, NB, P])
        v_sb = sb("v_sb", [P, NB, P])
        qstack = sb("qstack", [P, G, NB, J, P], F32R)
        kstack = sb("kstack", [P, G, NB, P], F32R)
        vpad = sb("vpad", [P, 2, H, P])
        m_nat = sb("m_nat", [P, NB, H])
        m_exp = sb("m_exp", [P, 2, H, DH])
        mt = sb("mt", [P, NB, P], F32R)
        probs = sb("probs", [P, 2, J, P])
        x2 = sb("x2", [P, NB, P])

        x3 = sb("x3", [P, NB, P])
        x2_hi = sb("x2_hi", [P, NB, P], F32R)
        x2_lo = sb("x2_lo", [P, NB, P], F32R)
        h_hi = sb("h_hi", [P, 2, 512], F32R)
        h_lo = sb("h_lo", [P, 2, 512], F32R)
        h_ex = sb("h_ex", [P, 2, FC, P])
        outs = sb("outs", [P, 5, NB, P])
        hid = sb("hid", [P, 2, NB])
        gate = sb("gate", [P, 4, NB])
        gmax = sb("gmax", [P, NB])

        consts_in = sem("consts_in")
        stage_in = sem("stage_in")
        x_in = sem("x_in")
        s_in = sem("s_in")
        ring_in = [sem(f"ring_in{k}") for k in range(RING)]
        q_stacked = sem("q_stacked")
        k_stacked = sem("k_stacked")
        m_stacked = sem("m_stacked")
        stored = sem("stored")
        setup_dve = sem("setup_dve")
        setup_act = sem("setup_act")
        setup_pe = sem("setup_pe")
        setup_pool = sem("setup_pool")
        setup_gate = sem("setup_gate")
        setup_gate_exp = sem("setup_gate_exp")
        setup_chain = sem("setup_chain")
        pe_lora = sem("pe_lora")
        pe_proj = sem("pe_proj")
        pe_self = sem("pe_self")
        pe_s = sem("pe_s")
        pe_mt = sem("pe_mt")
        pe_st = sem("pe_st")
        pe_av = sem("pe_av")
        pe_wo = sem("pe_wo")
        pe_f1 = sem("pe_f1")
        pe_f2 = sem("pe_f2")
        pe_hid = sem("pe_hid")
        pe_logit = sem("pe_logit")
        act_s2 = sem("act_s2")
        act_x1 = sem("act_x1")
        act_proj = sem("act_proj")
        act_kh = sem("act_kh")
        act_self = sem("act_self")
        act_exp = sem("act_exp")
        act_ps = sem("act_ps")
        act_x2 = sem("act_x2")
        act_x3 = sem("act_x3")
        act_unit = sem("act_unit")
        act_out = sem("act_out")
        act_hid = sem("act_hid")
        act_gate = sem("act_gate")
        dve_adapt = sem("dve_adapt")
        dve_x1 = sem("dve_x1")
        dve_x1_lo = sem("dve_x1_lo")
        dve_s2_lo = sem("dve_s2_lo")
        dve_q = sem("dve_q")
        dve_kf = sem("dve_kf")
        dve_k_lo = sem("dve_k_lo")
        dve_max = sem("dve_max")
        dve_mexp = sem("dve_mexp")
        dve_mt = sem("dve_mt")
        dve_sub = sem("dve_sub")
        dve_pre = sem("dve_pre")
        dve_att = sem("dve_att")
        dve_x2 = sem("dve_x2")
        dve_x2_lo = sem("dve_x2_lo")
        dve_lo = sem("dve_lo")
        dve_logit = sem("dve_logit")
        dve_mix2 = sem("dve_mix2")
        dve_x3_lo = sem("dve_x3_lo")
        dve_exmix = sem("dve_exmix")
        dve_mix3 = sem("dve_mix3")
        dve_tables = sem("dve_tables")
        dve_fin = sem("dve_fin")
        dve_gate = sem("dve_gate")
        dve_term = sem("dve_term")
        pool_vpad = sem("pool_vpad")
        pool_pv = sem("pool_pv")

        CONSTS = [(const[:], consts), (ints[:, 0], lens), (ints[:, 1], labels), (ints[:, 2], langs),
                  (gv[:], gate_vecs), (wraw[:], wqkvo), (vec[:], vecs), (lora_a[:], loraA),
                  (lora_be[:], loraBe), (g1_sb[:], g1), (g2_sb[:], g2r), (gw1_sb[:], gw1), (gw2_sb[:], gw2r)]

        def wait(eng, s, value):
            if isinstance(value, int) and value <= 0:
                return
            eng.wait_ge(s, value)

        def per_key(ap, parts=P):
            return ap.unsqueeze(2).broadcast_to([parts, NB, P])

        def walk(handlers, i, j):
            for who, name, k in SCHEDULE:
                group = i if who == "a" else j
                if group is not None and name in handlers:
                    handlers[name](group, k)

        def run(handlers, engine, before=None):
            walk(handlers, 0, None)
            walk(handlers, 1, 0)
            with engine.Fori(2, groups) as i:
                walk(handlers, i, i - 1)
            walk(handlers, None, groups - 1)

        block = ctx.enter_context(nc.Block())

        @block.sync
        def _(sp):
            for dst, src in CONSTS:
                sp.dma_start(dst, src).then_inc(consts_in, 16)
            for e in range(NS):
                sp.dma_start(ring[:, e], shared[:, e]).then_inc(stage_in, 16)
            sp.wait_ge(setup_pool, 2)
            sp.wait_ge(setup_act, 4)

            def wait_first(s, value):
                wait(sp, s, value)
                sp.wait_ge(consts_in, 16 * len(CONSTS))

            def fetch(group, n, s=None, value=None):
                which, b = divmod(n, NB)
                label = sp.value_load(ints[0:1, 1, bass.ds(group * NB + b, 1)], min_val=0, max_val=TYPES - 1)
                if which == 2:
                    label = label + 1
                src = experts[which][bass.ds(label, 1)].rearrange("o p f -> (o p) f")
                if s is not None:
                    wait_first(s, value)
                sp.dma_start(ring[:, n % RING], src).then_inc(ring_in[n % RING], 16)

            def load(i, _):
                wait_first(dve_x2, i)
                sp.dma_start(x1[:], xT[bass.ds(i, 1)].rearrange("o p b t -> (o p) b t")).then_inc(x_in, 16)
                wait_first(dve_s2_lo, i)
                sp.dma_start(s2[:], sT[bass.ds(i, 1)].rearrange("o p b t -> (o p) b t")).then_inc(s_in, 16)
                if isinstance(i, int) and i == 0:
                    sp.wait_ge(setup_dve, 1)
                    for n in range(RING):
                        fetch(0, n)

            def refill(j, u):
                done = u - 2
                if done in EXPERT_UNITS:
                    n = EXPERT_UNITS.index(done) + RING
                    last = isinstance(j, int) and j == groups - 1
                    if n < len(EXPERT_UNITS):
                        fetch(j, n, pe_f2, UNITS * j + done + 1)
                    elif not last:
                        fetch(j + 1, n - len(EXPERT_UNITS), pe_f2, UNITS * j + done + 1)

            def exmix(j, _):
                refill(j, UNITS)
                refill(j, UNITS + 1)

            def mix3(j, _):
                wait_first(dve_mix3, j + 1)
                sp.dma_start(out[bass.ds(j, 1)].rearrange("o p b t -> (o p) b t"), x3[:]).then_inc(stored, 16)

            def stack(i, _):
                wait(sp, pe_av, 16 * i)
                wait(sp, act_proj, 5 * i + 3)
                wait(sp, dve_q, 2 * i + 1)
                for part, src in enumerate((s2_hi, s2_hi, s2_lo)):
                    for h in range(H):
                        g, jj = divmod(h, J)
                        row = 32 * part + DH * jj
                        sp.dma_start(qstack[row:row + DH, g, :, jj, :].bitcast(F32),
                                     src[DH * h:DH * h + DH].bitcast(F32)).then_inc(q_stacked, 16)
                wait(sp, act_kh, i + 1)
                wait(sp, dve_k_lo, i + 1)
                for part, src in enumerate((x1_hi, x1_lo, x1_hi)):
                    for g in range(G):
                        sp.dma_start(kstack[32 * part:32 * part + 32, g].bitcast(F32),
                                     src[32 * g:32 * g + 32].bitcast(F32)).then_inc(k_stacked, 16)

            def mq(i, _):
                wait(sp, dve_mt, i + 1)
                for h in range(H):
                    g, jj = divmod(h, J)
                    row = 96 + DH * jj
                    sp.dma_start(qstack[row:row + 1, g, :, jj, :].bitcast(F32),
                                 mt[DH * h:DH * h + 1].bitcast(F32)).then_inc(m_stacked, 16)

            run({"load": load, "unit": refill, "exmix": exmix, "stack": stack, "mq": mq, "mix3": mix3}, sp)
            sp.wait_ge(stored, 16 * groups)

        Q_DMAS, K_DMAS, M_DMAS = 3 * H * 16, 3 * G * 16, H * 16

        @block.gpsimd
        def _(pool):
            nc.gpsimd.memset(qstack[:].bitcast(F32), 0.0).then_inc(setup_pool, 1)
            nc.gpsimd.memset(vpad[:], 0.0).then_inc(setup_pool, 1)
            pool.wait_ge(setup_pool, 2)

            def stack(i, _):
                wait(pool, act_proj, 5 * i + 5)
                pad(i, 0)
                pad(i, 1)

            def E(i, k):
                if k in (G, 2 * G):
                    pad(i, k // G + 1)

            def pad(i, b):
                wait(pool, dve_pre, i + 1)
                wait(pool, pe_av, 16 * i + 4 * (b - 1))
                v = v_sb[:, b].rearrange("p (h d) -> p h d", h=H)
                half = H // 2
                for t in range(2):
                    mask = mask_g[:, b:b + 1].unsqueeze(2).broadcast_to([P, half, DH])
                    nc.gpsimd.tensor_tensor(diagonal(vpad, b % 2, half * t, 64 * t),
                                            v[:, half * t:half * t + half], mask, ALU.mult)
                    last = nc.gpsimd.tensor_copy(diagonal(vpad, b % 2, half * t, 64 * (1 - t)), mask)
                last.then_inc(pool_vpad, 1)

            def diagonal(tile, buf, h0, c0):
                ap = tile[:, buf, h0:h0 + H // 2, c0:c0 + DH].copy()
                dims = [list(d) for d in ap.ap]
                dims[1][0] = dims[1][0] + DH
                return bass.AP(tensor=ap.tensor, offset=ap.offset, ap=dims)

            def fin(i, _):
                wait(pool, act_ps, i + 1)
                wait(pool, act_proj, 5 * i + 2)
                nc.gpsimd.tensor_tensor(v_self[:], v_self[:], kf[:], ALU.mult).then_inc(pool_pv, 1)

            run({"stack": stack, "E": E, "fin": fin}, pool)

        def mm3(out_ap, a_hi, a_lo, b_hi, b_lo, start, stop):
            nc.tensor.matmul(out_ap, a_hi, b_hi, start=start, stop=False)
            nc.tensor.matmul(out_ap, a_hi, b_lo, start=False, stop=False)
            return nc.tensor.matmul(out_ap, a_lo, b_hi, start=False, stop=stop)

        def flat(tile):
            return tile[:].rearrange("p b t -> p (b t)")

        @block.tensor
        def _(pe):
            pe.wait_ge(consts_in, 16 * len(CONSTS))
            for k, (w, v) in enumerate(((0, 5), (1, 4), (1, 5), (3, 2))):
                last = nc.tensor.matmul(bank_a[0][:, k:k + 1], wraw[:, w], vec[:, v:v + 1], start=True, stop=True)
            last.then_inc(setup_pe, 1)
            pe.wait_ge(setup_act, 4)
            pe.wait_ge(setup_dve, 2)

            def lora1(i, _):
                wait(pe, x_in, 16 * (i + 1))
                wait(pe, dve_att, 4 * i)
                nc.tensor.matmul(bank_a[2][0:LR], lora_a[:], flat(x1), start=True, stop=True).then_inc(pe_lora, 1)

            def lora2(i, _):
                wait(pe, dve_adapt, 2 * (i + 1))
                nc.tensor.matmul(bank_a[3][:], lora_be[:], flat(adapt), start=True, stop=True).then_inc(pe_lora, 1)

            def proj(i, _):
                wait(pe, act_s2, i + 1)
                wait(pe, dve_s2_lo, i + 1)
                wait(pe, dve_x2, i)
                wait(pe, act_exp, 16 * i)
                for bank, w in ((0, 1), (1, 2), (2, 0)):
                    mm3(bank_a[bank][:], w_hi[:, w], w_lo[:, w], flat(s2_hi), flat(s2_lo),
                        True, True).then_inc(pe_proj, 1)
                wait(pe, act_x1, i + 1)
                wait(pe, dve_x1_lo, i + 1)
                mm3(bank_a[3][:], w_hi[:, 1], w_lo[:, 1], flat(x1_hi), flat(x1_lo), True, True).then_inc(pe_proj, 1)
                wait(pe, act_proj, 5 * i + 2)
                for b in range(NB):
                    last = nc.tensor.matmul(bank_a[1][:, b * P:b * P + P], x1[:, b], wraw[:, 2],
                                            start=True, stop=True)
                last.then_inc(pe_proj, 1)

            def self_(i, _):
                wait(pe, dve_q, 2 * i + 2)
                nc.tensor.matmul(bank_a[0][:], head_sum, flat(k_self), start=True, stop=True).then_inc(pe_self, 1)

            def S(i, b):
                if b == 0:
                    wait(pe, q_stacked, Q_DMAS * (i + 1))
                    wait(pe, k_stacked, K_DMAS * (i + 1))
                    wait(pe, act_self, i + 1)
                    wait(pe, act_proj, 5 * i + 5)
                for g in range(G):
                    n = G * b + g
                    if n >= 2:
                        wait(pe, dve_max, 16 * i + n - 1)
                    for jj in range(J):
                        last = nc.tensor.matmul(bank_a[n % 2][:, jj * P:jj * P + P], qstack[0:96, g, b, jj],
                                                kstack[0:96, g, b], start=True, stop=True)
                    last.then_inc(pe_s, 1)
                if b:
                    turn_max(i, b - 1)

            def turn_max(i, b):
                wait(pe, dve_mexp, NB * i + b + 1)
                last = nc.tensor.transpose(bank_a[2][:, b * P:b * P + P],
                                           m_exp[:, b % 2].rearrange("p h d -> p (h d)"), ident)
                last.then_inc(pe_mt, 1)

            def mq(i, _):
                turn_max(i, NB - 1)

            def av(i, k):
                b, g = divmod(k, G)
                wait(pe, act_exp, 16 * i + k + 1)
                if g == 0:
                    wait(pe, pool_vpad, NB * i + b + 1)
                    if b == 0:
                        wait(pe, dve_mt, i + 1)
                for jj in range(J):
                    h = J * g + jj
                    half, hh = divmod(h, H // 2)
                    last = nc.tensor.matmul(bank_a[2 + half][:, b * P:b * P + P], vpad[:, b % 2, h],
                                            probs[:, k % 2, jj], start=(hh == 0), stop=(hh == H // 2 - 1))
                last.then_inc(pe_av, 1)

            def E(i, k):
                b, g = divmod(k, G)
                if k == 0:
                    wait(pe, m_stacked, M_DMAS * (i + 1))
                    wait(pe, dve_max, 16 * (i + 1))
                if k >= 2:
                    wait(pe, act_exp, 16 * i + k - 1)
                nc.tensor.matmul(bank_a[k % 2][:], kstack[:, g, b],
                                 qstack[:, g, b].rearrange("p j t -> p (j t)"),
                                 start=True, stop=True).then_inc(pe_st, 1)
                if k:
                    av(i, k - 1)

            def Eend(i, _):
                av(i, NB * G - 1)

            def wo(i, _):
                wait(pe, dve_att, 4 * (i + 1))
                nc.tensor.matmul(bank_a[0][:], wraw[:, 3], flat(kf), start=True, stop=True).then_inc(pe_wo, 1)

            def f1(j, u):
                o, c = divmod(u, 4)
                layer, kind, e = OUTS[o]
                if u == 0:
                    wait(pe, act_x2, j + 1)
                    wait(pe, dve_x2_lo, j + 1)
                if u == L3_FIRST:
                    wait(pe, act_x3, j + 1)
                    wait(pe, dve_x3_lo, j + 1)
                wait(pe, act_unit, UNITS * j + u - 1)
                wait(pe, dve_lo, NSHARED * j + SHARED_BEFORE[u - 1] if u else NSHARED * j)
                bank = bank_h[u % 2]
                if kind == "shared":
                    last = mm3(bank[:], sh_hi[:, e, c * P:c * P + P], sh_lo[:, e, c * P:c * P + P],
                               flat(x2_hi), flat(x2_lo), True, True)
                else:
                    n = EXPERT_UNITS.index(u)
                    wait(pe, ring_in[n % RING], 16 * (2 * j + n // RING + 1))
                    src = (x2 if layer == 2 else x3)[:, c]
                    for cc in range(FC):
                        last = nc.tensor.matmul(bank[:, cc * P:cc * P + P], ring[:, n % RING, cc * P:cc * P + P],
                                                src, start=True, stop=True)
                last.then_inc(pe_f1, 1)

            free_o = [(act_out, NO, 0), (dve_logit, 2, 0), (act_out, NO, 1), (act_out, NO, 3),
                      (dve_logit, 2, 1), (act_out, NO, 4), (act_out, NO, 5), (act_out, NO, 6)]
            slot_o = [0, 1, 0, 0, 1, 0, 1, 0]

            def f2(j, u):
                o, c = divmod(u, 4)
                _, kind, e = OUTS[o]
                bank = bank_o[slot_o[o]]
                if c == 0:
                    s, per, n = free_o[o]
                    wait(pe, s, per * j + n)
                wait(pe, act_unit, UNITS * j + u + 1)
                if kind == "shared":
                    wait(pe, dve_lo, NSHARED * j + SHARED_BEFORE[u + 1])
                    w = slice(F + c * P, F + c * P + P)
                    last = mm3(bank[:], sh_hi[:, e, w], sh_lo[:, e, w], h_hi[:, u % 2], h_lo[:, u % 2],
                               c == 0, c == FC - 1)
                else:
                    n = EXPERT_UNITS.index(u)
                    for cc in range(FC):
                        last = nc.tensor.matmul(bank[:, c * P:c * P + P],
                                                ring[:, n % RING, F + cc * P:F + cc * P + P], h_ex[:, u % 2, cc],
                                                start=(cc == 0), stop=(cc == FC - 1))
                last.then_inc(pe_f2, 1)

            def unit(j, u):
                f1(j, u)
                if u not in (0, L3_FIRST):
                    f2(j, u - 1)

            def l2end(j, _):
                f2(j, L3_FIRST - 1)

            def l3end(j, _):
                f2(j, UNITS - 1)

            def hid_(j, layer):
                if layer == 0:
                    wait(pe, act_out, NO * j + 3)
                    terms = [(g1_sb, 0, 0), (g1_sb, 1, 1), (g1_sb, 2, 2)]
                else:
                    wait(pe, act_out, NO * j + 8)
                    wait(pe, dve_exmix, 2 * j + 2)
                    terms = [(gw1_sb, 0, 3), (gw1_sb, 1, 0), (gw1_sb, 2, 1), (gw1_sb, 3, 2)]
                for n, (w, row, o) in enumerate(terms):
                    last = nc.tensor.matmul(bank_o[1][:, 0:NB], w[:, row], outs[:, o, :, 0],
                                            start=(n == 0), stop=(n == len(terms) - 1))
                last.then_inc(pe_hid, 1)

            def logit(j, layer):
                wait(pe, act_hid, 2 * j + layer + 1)
                for n in range(3 + layer):
                    last = nc.tensor.matmul(bank_o[1][:, 8 + NB * n:8 + NB * n + NB],
                                            (gw2_sb if layer else g2_sb)[:, n], hid[:, layer],
                                            start=True, stop=True)
                last.then_inc(pe_logit, 1)

            run({"lora1": lora1, "lora2": lora2, "proj": proj, "self": self_, "S": S, "mq": mq, "E": E,
                 "Eend": Eend, "wo": wo, "unit": unit, "l2end": l2end, "l3end": l3end, "hid": hid_,
                 "logit": logit}, pe)

        @block.scalar
        def _(act):
            def high(dst, src):
                return nc.scalar.activation(dst, src, ACT.Copy)

            act.wait_ge(consts_in, 16 * len(CONSTS))
            act.wait_ge(setup_gate, 1)
            nc.scalar.activation(gv[:], gv[:], ACT.Exp).then_inc(setup_gate_exp, 1)
            act.wait_ge(stage_in, 16 * NS)
            for e in range(NS):
                last = high(sh_hi[:, e], ring[:, e])
            last.then_inc(setup_act, 1)
            nc.scalar.activation(w_hi[:, 0], wraw[:, 0], ACT.Copy, scale=SCALE).then_inc(setup_act, 1)
            high(w_hi[:, 1:3], wraw[:, 1:3]).then_inc(setup_act, 1)
            nc.scalar.activation(kstack[96:128].rearrange("p g b t -> p (g b t)"),
                                 shift_row[96:128].broadcast_to([32, G * NB * P]), ACT.Copy).then_inc(setup_act, 1)

            def lora1(i, _):
                wait(act, s_in, 16 * (i + 1))
                wait(act, q_stacked, Q_DMAS * i)
                high(s2_hi[:], s2[:]).then_inc(act_s2, 1)

            def lora2(i, _):
                wait(act, dve_x1, i + 1)
                wait(act, k_stacked, K_DMAS * i)
                high(x1_hi[:], x1[:]).then_inc(act_x1, 1)

            def proj(i, _):
                wait(act, setup_dve, 2) if isinstance(i, int) and i == 0 else None
                wait(act, dve_att, 4 * i)
                wait(act, pe_proj, 5 * i + 1)
                nc.scalar.activation(flat(k_self), bank_a[0][:], ACT.Identity, bias=bias[:, 2:3]).then_inc(act_proj, 1)
                wait(act, pe_proj, 5 * i + 2)
                nc.scalar.activation(flat(v_self), bank_a[1][:], ACT.Copy).then_inc(act_proj, 1)
                wait(act, pe_proj, 5 * i + 3)
                wait(act, dve_s2_lo, i + 1)
                nc.scalar.activation(flat(s2_hi), bank_a[2][:], ACT.Identity, bias=bias[:, 0:1]).then_inc(act_proj, 1)
                wait(act, pe_proj, 5 * i + 4)
                wait(act, pe_wo, i)
                nc.scalar.activation(flat(kf), bank_a[3][:], ACT.Identity, bias=bias[:, 1:2]).then_inc(act_proj, 1)
                wait(act, pe_proj, 5 * i + 5)
                wait(act, pool_vpad, NB * i)
                nc.scalar.activation(flat(v_sb), bank_a[1][:], ACT.Copy).then_inc(act_proj, 1)
                wait(act, dve_kf, i + 1)
                high(x1_hi[:], kf[:]).then_inc(act_kh, 1)

            def self_(i, _):
                wait(act, pe_self, i + 1)
                nc.scalar.activation(flat(s_self), bank_a[0][:], ACT.Copy).then_inc(act_self, 1)

            def E(i, k):
                wait(act, pe_st, 16 * i + k + 1)
                if k >= 2:
                    wait(act, pe_av, 16 * i + k - 1)
                nc.scalar.activation(probs[:, k % 2].rearrange("p j t -> p (j t)"), bank_a[k % 2][:],
                                     ACT.Exp).then_inc(act_exp, 1)

            def Eend(i, _):
                wait(act, dve_sub, i + 1)
                nc.scalar.activation(kf[:], kf[:], ACT.Exp).then_inc(act_ps, 1)

            def wo(i, _):
                wait(act, dve_x2, i + 1)
                wait(act, pe_f1, UNITS * (i - 1) + 24 if not (isinstance(i, int) and i == 0) else 0)
                high(x2_hi[:], x2[:]).then_inc(act_x2, 1)

            def unit(j, u):
                wait(act, pe_f1, UNITS * j + u + 1)
                if u >= 2:
                    wait(act, pe_f2, UNITS * j + u - 1)
                elif not (isinstance(j, int) and j == 0):
                    wait(act, pe_f2, UNITS * j)
                kind = OUTS[u // 4][1]
                dst = h_hi[:, u % 2] if kind == "shared" else h_ex[:, u % 2].rearrange("p c t -> p (c t)")
                nc.scalar.activation(dst, bank_h[u % 2][:], ACT.Relu).then_inc(act_unit, 1)
                if u % 4 == 0 and u not in (0, L3_FIRST):
                    take(j, u // 4 - 1)

            place_o = [0, 1, 2, 0, 1, 2, 3, 4]
            slot_o = [0, 1, 0, 0, 1, 0, 1, 0]

            def take(j, o):
                wait(act, pe_f2, UNITS * j + 4 * o + 4)
                if OUTS[o][0] == 3:
                    wait(act, dve_mix2, j + 1)
                elif o == 0:
                    wait(act, dve_mix3, j)
                nc.scalar.activation(outs[:, place_o[o]].rearrange("p b t -> p (b t)"), bank_o[slot_o[o]][:],
                                     ACT.Copy).then_inc(act_out, 1)

            def l2end(j, _):
                take(j, 2)

            def l3end(j, _):
                take(j, 7)

            def hid_(j, layer):
                wait(act, pe_hid, 2 * j + layer + 1)
                nc.scalar.activation(hid[:, layer], bank_o[1][:, 0:NB], ACT.Relu).then_inc(act_hid, 1)

            def soft(j, layer):
                wait(act, dve_logit, 2 * j + layer + 1)
                n = 3 + layer
                nc.scalar.activation(gate[:, 0:n], gate[:, 0:n], ACT.Exp).then_inc(act_gate, 1)

            def mix2(j, _):
                wait(act, dve_mix2, j + 1)
                wait(act, pe_f1, UNITS * j + L3_FIRST)
                high(x2_hi[:], x3[:]).then_inc(act_x3, 1)

            run({"lora1": lora1, "lora2": lora2, "proj": proj, "self": self_, "E": E, "Eend": Eend, "wo": wo,
                 "unit": unit, "l2end": l2end, "l3end": l3end, "hid": hid_, "soft": soft, "mix2": mix2}, act)

        @block.vector
        def _(dve):
            def low(dst, src, hi):
                return nc.vector.tensor_tensor(dst, src, hi.bitcast(F32), ALU.subtract)

            class Chain:
                def __init__(self, s):
                    self.s, self.n, self.base = s, 0, 0

                def __call__(self, ins):
                    ins.then_inc(self.s, 1)
                    self.n += 1

                def settle(self):
                    dve.wait_ge(self.s, self.base + self.n)

            c = Chain(setup_chain)
            dve.wait_ge(consts_in, 16 * len(CONSTS))
            c(nc.vector.tensor_copy(lens_f[:], ints[:, 0]))
            c(nc.vector.tensor_copy(labels_f[:], ints[:, 1]))
            c(nc.vector.tensor_copy(langs_f[:], ints[:, 2]))
            c(nc.vector.tensor_reduce(gv_s[:], gv[:], AXX, ALU.max))
            c.settle()
            c(nc.vector.tensor_scalar(key_mask[:], lens_f[:], part_no, None, ALU.is_gt))
            c(nc.vector.tensor_scalar(lang_hot[:], langs_f[:], lang_no, None, ALU.is_equal))
            c(nc.vector.tensor_tensor(gv[:], gv[:], gv_s[:].unsqueeze(2).broadcast_to([P, TYPES, 4]), ALU.subtract))
            c.settle()
            nc.vector.tensor_scalar(gv[:], gv[:], 10.0, None, ALU.mult).then_inc(setup_gate, 1)
            dve.wait_ge(setup_gate_exp, 1)
            c(nc.vector.tensor_reduce(gv_s[:], gv[:], AXX, ALU.add))
            c.settle()
            c(nc.vector.reciprocal(gv_s[:], gv_s[:]))
            c.settle()
            c(nc.vector.tensor_tensor(gv[:], gv[:], gv_s[:].unsqueeze(2).broadcast_to([P, TYPES, 4]), ALU.mult))
            c.settle()
            for k in range(2):
                c(nc.vector.tensor_scalar(wab[:, k], labels_f[:], 0.0, gv[:, 0, k:k + 1], ALU.is_equal, ALU.mult))
                for t in range(1, TYPES):
                    c(nc.vector.tensor_scalar(wab_t[:], labels_f[:], float(t), gv[:, t, t + k:t + k + 1],
                                              ALU.is_equal, ALU.mult))
                    c.settle()
                    c(nc.vector.tensor_tensor(wab[:, k], wab[:, k], wab_t[:], ALU.add))
                    c.settle()
            dve.wait_ge(setup_act, 1)
            for e in range(NS):
                last = low(sh_lo[:, e], ring[:, e], sh_hi[:, e])
            last.then_inc(setup_dve, 1)
            dve.wait_ge(setup_act, 3)
            nc.vector.scalar_tensor_tensor(w_lo[:, 0], wraw[:, 0], SCALE, w_hi[:, 0].bitcast(F32), ALU.mult,
                                           ALU.subtract)
            low(w_lo[:, 1:3], wraw[:, 1:3], w_hi[:, 1:3])
            dve.wait_ge(setup_pe, 1)
            c(nc.vector.tensor_scalar(bias[:, 0:1], bank_a[0][:, 0:1], vec[:, 0:1], SCALE, ALU.add, ALU.mult))
            c(nc.vector.tensor_scalar(bias[:, 1:3], bank_a[0][:, 1:3], vec[:, 1:2], None, ALU.add))
            c(nc.vector.tensor_scalar(bias[:, 3:4], bank_a[0][:, 3:4], vec[:, 3:4], None, ALU.add))
            c.settle()
            nc.vector.tensor_copy(bq_s[:], bias[:, 0:1]).then_inc(setup_dve, 1)
            dve.wait_ge(setup_dve, 2)

            def lora1(i, _):
                at = bass.ds(i * NB, NB)
                wait(dve, pool_vpad, NB * i)
                wait(dve, pe_lora, 2 * i)
                nc.vector.tensor_copy(hot_g[:], lang_hot[:, at]).then_inc(dve_tables, 1)
                nc.vector.tensor_copy(mask_g[:], key_mask[:, at]).then_inc(dve_pre, 1)
                nc.vector.tensor_copy(len_g[:], lens_f[:, at]).then_inc(dve_tables, 1)
                dve.wait_ge(dve_tables, 4 * i + 2)
                nc.vector.tensor_tensor(pad_key[:], key_no.unsqueeze(1).broadcast_to([P, NB, P]),
                                        per_key(len_g[:]), ALU.is_ge).then_inc(dve_tables, 1)
                nc.vector.tensor_copy(adapt[LR:LR + LANGS],
                                      per_key(hot_g[LR:LR + LANGS], LANGS)).then_inc(dve_adapt, 1)
                wait(dve, pe_lora, 2 * i + 1)
                nc.vector.tensor_tensor(adapt[0:LR], bank_a[2][0:LR].rearrange("p (b t) -> p b t", b=NB),
                                        per_key(hot_g[0:LR], LR), ALU.mult).then_inc(dve_adapt, 1)
                wait(dve, act_s2, i + 1)
                wait(dve, q_stacked, Q_DMAS * i)
                low(s2_lo[:], s2[:], s2_hi[:]).then_inc(dve_s2_lo, 1)

            def lora2(i, _):
                wait(dve, pe_lora, 2 * i + 2)
                nc.vector.tensor_tensor(flat(x1), flat(x1), bank_a[3][:], ALU.add).then_inc(dve_x1, 1)
                wait(dve, act_x1, i + 1)
                wait(dve, k_stacked, K_DMAS * i)
                low(x1_lo[:], x1[:], x1_hi[:]).then_inc(dve_x1_lo, 1)

            def proj(i, _):
                wait(dve, act_proj, 5 * i + 3)
                nc.vector.scalar_tensor_tensor(flat(s2_lo), bank_a[2][:], bq_s[:, 0:1], flat(s2_hi).bitcast(F32),
                                               ALU.add, ALU.subtract).then_inc(dve_q, 1)
                wait(dve, act_proj, 5 * i + 4)
                nc.vector.tensor_copy(k_first[:], kf[:, :, 0]).then_inc(dve_tables, 1)
                dve.wait_ge(dve_tables, 4 * i + 4)
                nc.vector.scalar_tensor_tensor(flat(k_self), bank_a[2][:], bq_s[:, 0:1], flat(k_self),
                                               ALU.add, ALU.mult).then_inc(dve_q, 1)
                for b in range(NB):
                    last = nc.vector.copy_predicated(kf[:, b], pad_key[:, b], k_first[:, b:b + 1].broadcast_to([P, P]))
                last.then_inc(dve_kf, 1)
                wait(dve, act_kh, i + 1)
                low(x1_lo[:], kf[:], x1_hi[:]).then_inc(dve_k_lo, 1)

            def S(i, b):
                for g in range(G):
                    n = G * b + g
                    wait(dve, pe_s, 16 * i + n + 1)
                    nc.vector.tensor_reduce(m_nat[:, b, J * g:J * g + J],
                                            bank_a[n % 2][:].rearrange("p (j t) -> p j t", j=J),
                                            AXX, ALU.max).then_inc(dve_max, 1)
                dve.wait_ge(dve_max, 16 * i + G * (b + 1))
                if b >= 2:
                    wait(dve, pe_mt, NB * i + b - 1)
                nc.vector.tensor_copy(m_exp[:, b % 2],
                                      m_nat[:, b].unsqueeze(2).broadcast_to([P, H, DH])).then_inc(dve_mexp, 1)

            def mq(i, _):
                wait(dve, pe_mt, NB * (i + 1))
                wait(dve, act_self, i + 1)
                wait(dve, m_stacked, M_DMAS * i)
                nc.vector.tensor_tensor(flat(mt), bank_a[2][:], flat(s_self), ALU.max).then_inc(dve_mt, 1)
                dve.wait_ge(dve_mt, i + 1)
                dve.wait_ge(dve_k_lo, i + 1)
                nc.vector.tensor_tensor(kf[:], s_self[:], mt[:].bitcast(F32), ALU.subtract).then_inc(dve_sub, 1)

            def fin(i, _):
                wait(dve, pe_av, 16 * (i + 1))
                wait(dve, act_ps, i + 1)
                ks, kff, vs = flat(k_self), flat(kf), flat(v_self)
                nc.vector.tensor_tensor(ks[0:64], bank_a[2][64:128], kff[0:64], ALU.add).then_inc(dve_fin, 1)
                nc.vector.tensor_tensor(ks[64:128], bank_a[3][0:64], kff[64:128], ALU.add).then_inc(dve_fin, 1)
                dve.wait_ge(dve_fin, 3 * i + 2)
                nc.vector.reciprocal(ks, ks).then_inc(dve_fin, 1)
                wait(dve, pool_pv, i + 1)
                nc.vector.tensor_tensor(vs[0:64], bank_a[2][0:64], vs[0:64], ALU.add).then_inc(dve_att, 1)
                nc.vector.tensor_tensor(vs[64:128], bank_a[3][64:128], vs[64:128], ALU.add).then_inc(dve_att, 1)
                dve.wait_ge(dve_att, 4 * i + 2)
                dve.wait_ge(dve_fin, 3 * i + 3)
                nc.vector.tensor_tensor(kff, vs, ks, ALU.mult).then_inc(dve_att, 2)

            def wo(i, _):
                wait(dve, pe_wo, i + 1)
                if not (isinstance(i, int) and i == 0):
                    wait(dve, pe_f1, UNITS * (i - 1) + 4)
                nc.vector.scalar_tensor_tensor(flat(x2), bank_a[0][:], bias[:, 3:4], flat(x1),
                                               ALU.add, ALU.add).then_inc(dve_x2, 1)
                wait(dve, act_x2, i + 1)
                low(x2_lo[:], x2[:], x2_hi[:]).then_inc(dve_x2_lo, 1)

            def unit(j, u):
                if OUTS[u // 4][1] == "shared":
                    wait(dve, act_unit, UNITS * j + u + 1)
                    nc.vector.scalar_tensor_tensor(h_lo[:, u % 2], bank_h[u % 2][:], 0.0,
                                                   h_hi[:, u % 2].bitcast(F32), ALU.max,
                                                   ALU.subtract).then_inc(dve_lo, 1)

            def logit(j, layer):
                wait(dve, pe_logit, 2 * j + layer + 1)
                n = 3 + layer
                lg = bank_o[1][:, 8:8 + NB * n].rearrange("p (w b) -> p w b", b=NB)
                nc.vector.tensor_reduce(gmax[:], lg.rearrange("p w b -> p b w"), AXX, ALU.max).then_inc(dve_gate, 1)
                dve.wait_ge(dve_gate, 8 * j + 4 * layer + 1)
                nc.vector.tensor_tensor(gate[:, 0:n], lg, gmax[:].unsqueeze(1).broadcast_to([P, n, NB]),
                                        ALU.subtract).then_inc(dve_logit, 1)

            def soft(j, layer):
                wait(dve, act_gate, 2 * j + layer + 1)
                n = 3 + layer
                base = 8 * j + 4 * layer
                nc.vector.tensor_reduce(gmax[:], gate[:, 0:n].rearrange("p w b -> p b w"), AXX,
                                        ALU.add).then_inc(dve_gate, 1)
                dve.wait_ge(dve_gate, base + 2)
                nc.vector.reciprocal(gmax[:], gmax[:]).then_inc(dve_gate, 1)
                dve.wait_ge(dve_gate, base + 3)
                nc.vector.tensor_tensor(gate[:, 0:n], gate[:, 0:n], gmax[:].unsqueeze(1).broadcast_to([P, n, NB]),
                                        ALU.mult).then_inc(dve_gate, 1)
                dve.wait_ge(dve_gate, base + 4)

            def add_term(dst, o, weight, acc, b, s):
                nc.vector.scalar_tensor_tensor(dst[:, b], outs[:, o, b], weight, acc[:, b],
                                               ALU.mult, ALU.add).then_inc(s, 1)

            def mix2(j, _):
                wait(dve, stored, 16 * j)
                wait(dve, act_out, NO * j + 3)
                for n in range(3):
                    for b in range(NB):
                        last_term = n == 2 and b == NB - 1
                        if n:
                            dve.wait_ge(dve_term, 24 * j + NB * (n - 1) + b + 1)
                        add_term(x3, n, gate[:, n, b:b + 1], x3 if n else x2, b, dve_term)
                dve.wait_ge(dve_term, 24 * j + 12)
                nc.vector.tensor_copy(wab_g[:], wab[:, :, bass.ds(j * NB, NB)]).then_inc(dve_mix2, 1)
                wait(dve, act_x3, j + 1)
                low(x2_lo[:], x3[:], x2_hi[:]).then_inc(dve_x3_lo, 1)

            def exmix(j, _):
                wait(dve, act_out, NO * j + 8)
                dve.wait_ge(dve_mix2, j + 1)
                for b in range(NB):
                    last = nc.vector.tensor_scalar(outs[:, 3, b], outs[:, 3, b], wab_g[:, 0, b:b + 1], None, ALU.mult)
                last.then_inc(dve_exmix, 1)
                dve.wait_ge(dve_exmix, 2 * j + 1)
                for b in range(NB):
                    last = nc.vector.scalar_tensor_tensor(outs[:, 3, b], outs[:, 4, b], wab_g[:, 1, b:b + 1],
                                                          outs[:, 3, b], ALU.mult, ALU.add)
                last.then_inc(dve_exmix, 1)

            def mix3(j, _):
                dve.wait_ge(dve_exmix, 2 * j + 2)
                wait(dve, pe_f1, UNITS * j + UNITS)
                for n, o in enumerate((3, 0, 1, 2)):
                    for b in range(NB):
                        if n:
                            dve.wait_ge(dve_term, 24 * j + 12 + NB * (n - 1) + b + 1)
                        ins = nc.vector.scalar_tensor_tensor(x3[:, b], outs[:, o, b], gate[:, n, b:b + 1],
                                                             x3[:, b], ALU.mult, ALU.add)
                        if n == 3 and b == NB - 1:
                            ins.then_inc(dve_mix3, 1)
                        elif n < 3:
                            ins.then_inc(dve_term, 1)

            run({"lora1": lora1, "lora2": lora2, "proj": proj, "S": S, "mq": mq, "fin": fin, "wo": wo,
                 "unit": unit, "logit": logit, "soft": soft, "mix2": mix2, "exmix": exmix, "mix3": mix3}, dve)


def kernel(x, itok_B_0_3, fside_BxSxS_0, itok_B_18_1004, itok_B_0_2, L0_cond_lora_A, L0_cond_lora_B,
           L0_cond_lang_embed, L1_cond_Wq, L1_cond_bq, L1_cond_Wk, L1_cond_bk, L1_cond_Wv, L1_cond_bv,
           L1_cond_Wo, L1_cond_bo, L1_cond_b_prev, L1_cond_b_self, L2_cond_wi, L2_cond_wo, L2_cond_swi,
           L2_cond_swo, L2_cond_g1, L2_cond_g2, L3_cond_expert_wi, L3_cond_expert_wo, L3_cond_share_wi,
           L3_cond_share_wo, L3_cond_gate_vecs, L3_cond_gate_w1, L3_cond_gate_w2):
    import concourse.bacc as bacc
    from concourse.bass_utils import run_bass_kernel_spmd

    a = np.asarray
    B = a(x).shape[0]
    groups = B // NB

    def turned(t):
        return np.ascontiguousarray(a(t).reshape(groups, NB, P, P).transpose(0, 3, 1, 2))

    def rows(t):
        return np.ascontiguousarray(np.broadcast_to(a(t).reshape(1, -1), (P, a(t).size)))

    def expert(wi, wo):
        wi, wo = a(wi), a(wo)
        n = wi.shape[0]
        wo = wo.reshape(n, FC, P, P).transpose(0, 2, 1, 3).reshape(n, P, FC * P)
        return np.ascontiguousarray(np.concatenate([wi, wo], axis=2))

    def cut(w, n):
        return np.ascontiguousarray(a(w).reshape(n, P, P).transpose(1, 0, 2))

    def spread(w):
        return np.ascontiguousarray(np.broadcast_to(a(w)[:, :, None], (P, a(w).shape[1], P)))

    p = np.arange(P)
    consts = np.zeros((P, 3 * P + 3), np.float32)
    consts[:, 0:P] = np.eye(P)
    consts[:, P:2 * P] = (p[:, None] // DH == p[None, :] // DH)
    consts[:, 2 * P:3 * P] = p[None, :]
    consts[:, 3 * P] = p
    consts[:, 3 * P + 1] = np.where(p < LR, p // RANK, p - LR)
    consts[:, 3 * P + 2] = np.where((p >= 96) & (p % DH == 0), -1, 0)

    shared = np.concatenate([expert(L2_cond_swi, L2_cond_swo), expert(L3_cond_share_wi, L3_cond_share_wo)])
    loraB = a(L0_cond_lora_B).transpose(0, 2, 1).reshape(LR, P)
    arrays = {
        "xT": turned(x), "sT": turned(fside_BxSxS_0),
        "lens": rows(itok_B_18_1004), "labels": rows(itok_B_0_2), "langs": rows(itok_B_0_3),
        "loraA": np.ascontiguousarray(a(L0_cond_lora_A).reshape(LR, P).T),
        "loraBe": np.concatenate([loraB, a(L0_cond_lang_embed)]),
        "wqkvo": np.ascontiguousarray(np.stack([a(L1_cond_Wq), a(L1_cond_Wk), a(L1_cond_Wv), a(L1_cond_Wo)], 1)),
        "vecs": np.ascontiguousarray(np.stack([a(v).reshape(P) for v in (
            L1_cond_bq, L1_cond_bk, L1_cond_bv, L1_cond_bo, L1_cond_b_prev, L1_cond_b_self)], 1)),
        "shared": np.ascontiguousarray(shared.transpose(1, 0, 2)),
        "experts2": expert(L2_cond_wi, L2_cond_wo), "experts3": expert(L3_cond_expert_wi, L3_cond_expert_wo),
        "g1": cut(L2_cond_g1, 3), "g2r": spread(L2_cond_g2),
        "gw1": cut(L3_cond_gate_w1, 4), "gw2r": spread(L3_cond_gate_w2),
        "gate_vecs": rows(L3_cond_gate_vecs).reshape(P, TYPES, 4),
        "consts": consts,
    }
    nc = bacc.Bacc("TRN2", target_bir_lowering=False, num_devices=1)
    args = [nc.dram_tensor(n, v.shape, mybir.dt.from_np(v.dtype), kind="ExternalInput").ap()
            for n, v in arrays.items()]
    out = nc.dram_tensor("out", (groups, P, NB, P), F32, kind="ExternalOutput").ap()
    cond_resid_kernel(nc, *args, out)
    r = run_bass_kernel_spmd(nc, [arrays], core_ids=[0])
    got = r.results[0]["out"]
    return np.ascontiguousarray(np.asarray(got).transpose(0, 2, 3, 1).reshape(B, P, P))
```

```python
from contextlib import ExitStack

import numpy as np

import concourse.bass as bass
from concourse import mybir

ALU = mybir.AluOpType
ACT = mybir.ActivationFunctionType
AXX = mybir.AxisListType.X
F32 = mybir.dt.float32
F32R = mybir.dt.float32r
I32 = mybir.dt.int32
U8 = mybir.dt.uint8

P = 128
NB = 4
H = 16
DH = P // H
G = 4
J = H // G
FC = 4
LANGS, RANK = 4, 16
LR = LANGS * RANK
TYPES = 3
SCALE = float(np.float32(1.0) / np.sqrt(np.float32(DH)))
RING = 8

OUTS = [(2, "shared", 0), (2, "expert", 0), (2, "shared", 1),
        (3, "shared", 2), (3, "shared", 3), (3, "shared", 4), (3, "expert", 1), (3, "expert", 2)]
TILE = (0, 1, 2, 3, 4, 5, 1, 0)
MIX2 = (1, 0, 2)
MIX3 = (1, 3, 4, 5)
UNITS = 4 * len(OUTS)
L3_FIRST = 12
NO = len(OUTS)
EXPERT_UNITS = [4 * o + b for o, (_, kind, _) in enumerate(OUTS) if kind == "expert" for b in range(NB)]
NE = len(EXPERT_UNITS)
SHARED_BEFORE = [sum(OUTS[v // 4][1] == "shared" for v in range(u)) for u in range(UNITS + 1)]
NSHARED = SHARED_BEFORE[UNITS]
X2_EXPERTS = max(u for u in EXPERT_UNITS if u < L3_FIRST) + 1
LAST_SPLIT = max(u for u in range(UNITS) if OUTS[u // 4][1] == "shared") + 1


def make_schedule():
    a = lambda name, k=0: ("a", name, k)
    p = lambda name, k=0: ("p", name, k)
    f = lambda name, k=0: ("f", name, k)
    l = lambda name, k=0: ("l", name, k)
    after = {u: [] for u in range(UNITS)}
    for u, names in {
        1: [l("hid", 1)], 2: [l("logit", 1)], 3: [l("soft", 1)], 4: [l("mix3", 0)], 5: [l("mix3", 1)],
        6: [l("mix3", 2), a("mq")], 7: [l("mix3", 3)], 8: [a("self_w")],
        11: [a("E", 0), f("l2end"), a("E", 1), f("hid", 0), a("E", 2), a("E", 3), f("logit", 0), a("E", 4),
             a("E", 5), f("soft", 0), a("E", 6), a("E", 7), a("E", 8), f("mix2"), a("E", 9)],
        12: [p("load")], 13: [a("fin", 0)], 14: [a("rec", 0)], 15: [a("rec", 1)], 16: [a("att", 0)],
        17: [a("Eend"), a("fin", 1)], 18: [a("rec", 2)], 19: [a("rec", 3), a("att", 1), p("load_s")],
        20: [p("lora1")], 21: [a("wo")], 22: [p("lora2")], 23: [p("split_s")], 24: [a("split2"), p("proj")],
        25: [p("self"), p("stack")],
        31: [f("l3end"), f("exmix")],
    }.items():
        after[u] += names
    for n in range(NB * G):
        after[n // 2 if n < 8 else 4 + (n - 8) // 3].insert(0, a("S", n))
    for k in range(10, NB * G):
        after[12 + (k - 10)].insert(0, a("E", k))
    for u in after:
        after[u].sort(key=lambda s: (0, s[2]) if s[1] == "S" else (1, 0))
    steps = []
    for u in range(UNITS):
        steps += [f("unit", u), *after.get(u, [])]
    return steps


SCHEDULE = make_schedule()


def cond_resid_kernel(nc, xT, sT, lens, labels, langs, loraA, loraBe, wqkvo, vecs, shared, experts2,
                      experts3, g1, g2r, gw1, gw2r, gate_vecs, consts, q_parts, k_parts, m_parts, out):
    groups = xT.shape[0]
    NSEQ = groups * NB
    E2, E3 = experts2.shape[0], experts3.shape[0]
    NS = shared.shape[1]
    FW = shared.shape[2]
    F = FC * P
    experts = [experts2, experts3, experts3]

    with ExitStack() as ctx:
        def sb(name, shape, dt=F32):
            return ctx.enter_context(nc.sbuf_tensor(name, shape, dt))

        def ps(name, shape):
            return ctx.enter_context(nc.psum_tensor(name, shape, F32))

        def sem(name):
            return ctx.enter_context(nc.semaphore(name))

        bank_a = [ps(f"bank_a{k}", [P, 512]) for k in range(4)]
        bank_h = [ps(f"bank_h{k}", [P, 512]) for k in range(2)]
        bank_o = [ps(f"bank_o{k}", [P, 512]) for k in range(2)]

        ring = sb("ring", [P, RING, FW])
        sh_hi = sb("sh_hi", [P, NS, FW], F32R)
        sh_lo = sb("sh_lo", [P, NS, FW], F32R)
        wraw = sb("wraw", [P, 4, P])
        w_hi = sb("w_hi", [P, 3, P], F32R)
        w_lo = sb("w_lo", [P, 3, P], F32R)
        lora_a = sb("lora_a", [P, LR])
        lora_be = sb("lora_be", [LR + LANGS, P])
        g1_sb = sb("g1_sb", [P, 3, P])
        g2_sb = sb("g2_sb", [P, 3, P])
        gw1_sb = sb("gw1_sb", [P, 4, P])
        gw2_sb = sb("gw2_sb", [P, 4, P])
        vec = sb("vec", [P, 6])
        bias = sb("bias", [P, 4])
        bq_s = sb("bq_s", [P, 1])
        const = sb("const", [P, 3 * P + 3])
        ident = const[:, 0:P]
        head_sum = const[:, P:2 * P]
        key_no = const[:, 2 * P:3 * P]
        part_no = const[:, 3 * P:3 * P + 1]
        lang_no = const[:, 3 * P + 1:3 * P + 2]
        shift_row = const[:, 3 * P + 2:3 * P + 3]

        ints = sb("ints", [P, 3, NSEQ], I32)
        lens_f = sb("lens_f", [P, NSEQ])
        labels_f = sb("labels_f", [P, NSEQ])
        langs_f = sb("langs_f", [P, NSEQ])
        key_mask = sb("key_mask", [P, NSEQ])
        lang_hot = sb("lang_hot", [P, NSEQ])
        gv = sb("gv", [P, TYPES, 4])
        gv_s = sb("gv_s", [P, TYPES])
        wab = sb("wab", [P, 2, NSEQ])

        x0 = sb("x0", [P, NB, P])
        x1 = sb("x1", [P, NB, P])
        s2 = sb("s2", [P, NB, P])
        x1_hi = sb("x1_hi", [P, NB, P], F32R)
        x1_lo = sb("x1_lo", [P, NB, P], F32R)
        s2_hi = sb("s2_hi", [P, NB, P], F32R)
        s2_lo = sb("s2_lo", [P, NB, P], F32R)
        adapt = sb("adapt", [LR + LANGS, NB, P])
        hot_g = sb("hot_g", [P, NB])
        len_g = sb("len_g", [P, NB])
        mask_g = sb("mask_g", [P, NB])
        wab_g = sb("wab_g", [P, 2, NB])
        pad_key = sb("pad_key", [P, NB, P], U8)
        kf = sb("kf", [P, NB, P])
        k_first = sb("k_first", [P, NB])
        k_self = sb("k_self", [P, NB, P])
        v_self = sb("v_self", [P, NB, P])
        s_self = s2
        v_sb = sb("v_sb", [P, NB, P])
        qstack = sb("qstack", [P, G, NB, J, P], F32R)
        kstack = sb("kstack", [P, G, NB, P], F32R)
        vpad = sb("vpad", [P, 2, H, P])
        m_nat = sb("m_nat", [P, NB, H])
        m_exp = sb("m_exp", [P, 2, H, DH])
        mt = sb("mt", [P, NB, P], F32R)
        probs = sb("probs", [P, 2, J, P])
        x2 = sb("x2", [P, NB, P])
        wab_t = x2[:, 0, 0:NSEQ]

        x3 = sb("x3", [P, NB, P])
        x2_hi = sb("x2_hi", [P, NB, P], F32R)
        x2_lo = sb("x2_lo", [P, NB, P], F32R)
        h_hi = sb("h_hi", [P, 2, 512], F32R)
        h_lo = sb("h_lo", [P, 2, 512], F32R)
        h_ex = sb("h_ex", [P, 2, FC, P])
        outs = sb("outs", [P, max(TILE) + 1, NB, P])
        hid = sb("hid", [P, 2, NB])
        gate = sb("gate", [P, 4, NB])
        gmax = sb("gmax", [P, NB])

        consts_in = sem("consts_in")
        stage_in = sem("stage_in")
        x_in = sem("x_in")
        s_in = sem("s_in")
        ring_in = [sem(f"ring_in{k}") for k in range(RING)]
        q_saved = sem("q_saved")
        k_saved = sem("k_saved")
        m_saved = sem("m_saved")
        q_stacked = sem("q_stacked")
        k_stacked = sem("k_stacked")
        m_stacked = sem("m_stacked")
        stored = sem("stored")
        setup_dve = sem("setup_dve")
        setup_act = sem("setup_act")
        setup_pe = sem("setup_pe")
        setup_pool = sem("setup_pool")
        setup_gate = sem("setup_gate")
        setup_gate_exp = sem("setup_gate_exp")
        setup_chain = sem("setup_chain")
        pe_lora = sem("pe_lora")
        pe_proj = sem("pe_proj")
        pe_self = sem("pe_self")
        pe_s = sem("pe_s")
        pe_mt = sem("pe_mt")
        pe_st = sem("pe_st")
        pe_av = sem("pe_av")
        pe_wo = sem("pe_wo")
        pe_f1 = sem("pe_f1")
        pe_f2 = sem("pe_f2")
        pe_hid = sem("pe_hid")
        pe_logit = sem("pe_logit")
        act_s2 = sem("act_s2")
        act_x1 = sem("act_x1")
        act_proj = sem("act_proj")
        act_kh = sem("act_kh")
        act_self = sem("act_self")
        act_exp = sem("act_exp")
        act_ps = sem("act_ps")
        act_fin = sem("act_fin")
        act_x2 = sem("act_x2")
        act_x3 = sem("act_x3")
        act_unit = sem("act_unit")
        act_out = sem("act_out")
        act_hid = sem("act_hid")
        act_gate = sem("act_gate")
        dve_adapt = sem("dve_adapt")
        dve_x1 = sem("dve_x1")
        dve_x1_lo = sem("dve_x1_lo")
        dve_s2_lo = sem("dve_s2_lo")
        dve_q = sem("dve_q")
        dve_kf = sem("dve_kf")
        dve_k_lo = sem("dve_k_lo")
        dve_max = sem("dve_max")
        dve_mexp = sem("dve_mexp")
        dve_mt = sem("dve_mt")
        dve_sub = sem("dve_sub")
        dve_pre = sem("dve_pre")
        dve_rec = sem("dve_rec")
        dve_x2 = sem("dve_x2")
        dve_x2_lo = sem("dve_x2_lo")
        dve_lo = sem("dve_lo")
        dve_logit = sem("dve_logit")
        dve_mix2 = sem("dve_mix2")
        dve_x3_lo = sem("dve_x3_lo")
        dve_exmix = sem("dve_exmix")
        dve_mix3 = sem("dve_mix3")
        dve_tables = sem("dve_tables")
        dve_gate = sem("dve_gate")
        dve_term = sem("dve_term")
        pool_vpad = sem("pool_vpad")
        pool_pv = sem("pool_pv")
        pool_den = sem("pool_den")
        pool_num = sem("pool_num")
        pool_att = sem("pool_att")

        CONSTS = [(const[:], consts), (ints[:, 0], lens), (ints[:, 1], labels), (ints[:, 2], langs),
                  (gv[:], gate_vecs), (wraw[:], wqkvo), (vec[:], vecs), (lora_a[:], loraA),
                  (lora_be[:], loraBe), (g1_sb[:], g1), (g2_sb[:], g2r), (gw1_sb[:], gw1), (gw2_sb[:], gw2r)]

        def attended(b, half):
            c = (2 * (b % 2) + half) * P
            return bank_a[2 + b // 2][:, c:c + P]

        Q_DMAS, K_DMAS, M_DMAS = 3 * J * 16, 3 * 16, J * 16

        def wait(eng, s, value):
            if isinstance(value, int) and value <= 0:
                return
            eng.wait_ge(s, value)

        def flat(tile):
            return tile[:].rearrange("p b t -> p (b t)")

        def per_key(ap, parts=P):
            return ap.unsqueeze(2).broadcast_to([parts, NB, P])

        def walk(handlers, nxt, i, j, late):
            for who, name, k in SCHEDULE:
                group = {"p": nxt, "a": i, "f": j, "l": late}[who]
                if group is not None and name in handlers:
                    handlers[name](group, k)

        def run(handlers, engine):
            last = groups - 1
            walk(handlers, 0, None, None, None)
            walk(handlers, 1, 0, None, None)
            walk(handlers, 2, 1, 0, None)
            with engine.Fori(2, last) as i:
                walk(handlers, i + 1, i, i - 1, i - 2)
            walk(handlers, None, last, last - 1, last - 2)
            walk(handlers, None, None, last, last - 1)
            walk(handlers, None, None, None, last)

        block = ctx.enter_context(nc.Block())

        @block.sync
        def _(sp):
            for dst, src in CONSTS:
                sp.dma_start(dst, src).then_inc(consts_in, 16)
            for e in range(NS):
                sp.dma_start(ring[:, e], shared[:, e]).then_inc(stage_in, 16)
            sp.wait_ge(setup_pool, 2)
            sp.wait_ge(setup_act, 4)

            def wait_first(s, value):
                wait(sp, s, value)
                sp.wait_ge(consts_in, 16 * len(CONSTS))

            def fetch(group, n, s=None, value=None):
                which, b = divmod(n, NB)
                label = sp.value_load(ints[0:1, 1, bass.ds(group * NB + b, 1)], min_val=0, max_val=TYPES - 1)
                if which == 2:
                    label = label + 1
                src = experts[which][bass.ds(label, 1)].rearrange("o p f -> (o p) f")
                if s is not None:
                    wait_first(s, value)
                sp.dma_start(ring[:, n % RING], src).then_inc(ring_in[n % RING], 16)

            def load(i, _):
                wait_first(dve_x1, i)
                sp.dma_start(x0[:], xT[bass.ds(i, 1)].rearrange("o p b t -> (o p) b t")).then_inc(x_in, 16)

            def load_s(i, _):
                wait_first(pool_att, 2 * i)
                sp.dma_start(s2[:], sT[bass.ds(i, 1)].rearrange("o p b t -> (o p) b t")).then_inc(s_in, 16)
                if isinstance(i, int) and i == 0:
                    sp.wait_ge(setup_dve, 1)
                    for n in range(RING):
                        fetch(0, n)

            def refill(j, u):
                done = u - 2
                if done in EXPERT_UNITS:
                    n = EXPERT_UNITS.index(done)
                    last = isinstance(j, int) and j == groups - 1
                    if n < NE - RING:
                        fetch(j, n + RING, pe_f2, UNITS * j + done + 1)
                    elif not last:
                        fetch(j + 1, n if n < RING else n - RING, pe_f2, UNITS * j + done + 1)

            def exmix(j, _):
                refill(j, UNITS)
                refill(j, UNITS + 1)

            def mix3(j, n):
                if n < 3:
                    return
                wait_first(dve_mix3, j + 1)
                sp.dma_start(out[bass.ds(j, 1)].rearrange("o p b t -> (o p) b t"), x3[:]).then_inc(stored, 16)

            def stack(i, _):
                wait(sp, dve_q, 2 * i + 1)
                wait(sp, act_proj, 5 * i + 3)
                sp.dma_start(by_row(q_parts[0]), flat(s2_hi).bitcast(F32)).then_inc(q_saved, 16)
                sp.dma_start(by_row(q_parts[1]), flat(s2_lo).bitcast(F32)).then_inc(q_saved, 16)
                wait(sp, act_kh, i + 1)
                wait(sp, dve_k_lo, i + 1)
                sp.dma_start(by_row(k_parts[0]), flat(x1_hi).bitcast(F32)).then_inc(k_saved, 16)
                sp.dma_start(by_row(k_parts[1]), flat(x1_lo).bitcast(F32)).then_inc(k_saved, 16)
                wait(sp, q_saved, 32 * (i + 1))
                for part, src in enumerate((0, 0, 1)):
                    for jj in range(J):
                        row = 32 * part + DH * jj
                        sp.dma_start(qstack[row:row + DH, :, :, jj, :].bitcast(F32),
                                     q_parts[src, DH * jj:DH * jj + DH]).then_inc(q_stacked, 16)
                wait(sp, k_saved, 32 * (i + 1))
                for part, src in enumerate((0, 1, 0)):
                    sp.dma_start(kstack[32 * part:32 * part + 32].bitcast(F32),
                                 k_parts[src]).then_inc(k_stacked, 16)

            def by_row(parts):
                return parts.rearrange("r g b t -> g r (b t)")

            def mq(i, _):
                wait(sp, dve_mt, i + 1)
                sp.dma_start(by_row(m_parts), flat(mt).bitcast(F32)).then_inc(m_saved, 16)
                wait(sp, m_saved, 16 * (i + 1))
                for jj in range(J):
                    row = 96 + DH * jj
                    sp.dma_start(qstack[row:row + 1, :, :, jj, :].bitcast(F32),
                                 m_parts[DH * jj:DH * jj + 1]).then_inc(m_stacked, 16)

            run({"load": load, "load_s": load_s, "unit": refill, "exmix": exmix, "stack": stack, "mq": mq, "mix3": mix3}, sp)
            sp.wait_ge(stored, 16 * groups)


        @block.gpsimd
        def _(pool):
            nc.gpsimd.memset(qstack[:].bitcast(F32), 0.0).then_inc(setup_pool, 1)
            nc.gpsimd.memset(vpad[:], 0.0).then_inc(setup_pool, 1)
            pool.wait_ge(setup_pool, 2)

            def stack(i, _):
                wait(pool, act_proj, 5 * i + 5)
                pad(i, 0)
                pad(i, 1)

            def E(i, k):
                if k in (G, 2 * G):
                    pad(i, k // G + 1)

            def pad(i, b):
                wait(pool, dve_pre, i + 1)
                wait(pool, pe_av, 16 * i + 4 * (b - 1))
                v = v_sb[:, b].rearrange("p (h d) -> p h d", h=H)
                half = H // 2
                for t in range(2):
                    mask = mask_g[:, b:b + 1].unsqueeze(2).broadcast_to([P, half, DH])
                    nc.gpsimd.tensor_tensor(diagonal(vpad, b % 2, half * t, 64 * t),
                                            v[:, half * t:half * t + half], mask, ALU.mult)
                    last = nc.gpsimd.tensor_copy(diagonal(vpad, b % 2, half * t, 64 * (1 - t)), mask)
                last.then_inc(pool_vpad, 1)

            def diagonal(tile, buf, h0, c0):
                ap = tile[:, buf, h0:h0 + H // 2, c0:c0 + DH].copy()
                dims = [list(d) for d in ap.ap]
                dims[1][0] = dims[1][0] + DH
                return bass.AP(tensor=ap.tensor, offset=ap.offset, ap=dims)

            def self_w(i, _):
                wait(pool, act_ps, i + 1)
                wait(pool, act_proj, 5 * i + 2)
                nc.gpsimd.tensor_tensor(v_self[:], v_self[:], kf[:], ALU.mult).then_inc(pool_pv, 1)

            def fin(i, pair):
                two = slice(2 * pair, 2 * pair + 2)
                wait(pool, act_fin, 8 * i + 4 * pair + 2)
                nc.gpsimd.tensor_tensor(k_self[:, two], k_self[:, two], kf[:, two], ALU.add).then_inc(pool_den, 1)
                wait(pool, act_fin, 8 * i + 4 * pair + 4)
                wait(pool, pool_pv, i + 1)
                nc.gpsimd.tensor_tensor(s_self[:, two], s_self[:, two], v_self[:, two],
                                        ALU.add).then_inc(pool_num, 1)

            def att(i, pair):
                two = slice(2 * pair, 2 * pair + 2)
                wait(pool, dve_rec, 4 * i + 2 * (pair + 1))
                wait(pool, pool_num, 2 * i + pair + 1)
                nc.gpsimd.tensor_tensor(kf[:, two], s_self[:, two], k_self[:, two], ALU.mult).then_inc(pool_att, 1)

            run({"stack": stack, "E": E, "self_w": self_w, "fin": fin, "att": att}, pool)

        def mm3(out_ap, a_hi, a_lo, b_hi, b_lo, start, stop):
            nc.tensor.matmul(out_ap, a_hi, b_hi, start=start, stop=False)
            nc.tensor.matmul(out_ap, a_hi, b_lo, start=False, stop=False)
            return nc.tensor.matmul(out_ap, a_lo, b_hi, start=False, stop=stop)

        @block.tensor
        def _(pe):
            pe.wait_ge(consts_in, 16 * len(CONSTS))
            for k, (w, v) in enumerate(((0, 5), (1, 4), (1, 5), (3, 2))):
                last = nc.tensor.matmul(bank_a[0][:, k:k + 1], wraw[:, w], vec[:, v:v + 1], start=True, stop=True)
            last.then_inc(setup_pe, 1)
            pe.wait_ge(setup_act, 4)
            pe.wait_ge(setup_dve, 2)

            def lora1(i, _):
                wait(pe, x_in, 16 * (i + 1))
                wait(pe, act_fin, 8 * i)
                nc.tensor.matmul(bank_a[2][0:LR], lora_a[:], flat(x0), start=True, stop=True).then_inc(pe_lora, 1)

            def lora2(i, _):
                wait(pe, dve_adapt, 2 * (i + 1))
                nc.tensor.matmul(bank_a[3][:], lora_be[:], flat(adapt), start=True, stop=True).then_inc(pe_lora, 1)

            def proj(i, _):
                wait(pe, act_s2, i + 1)
                wait(pe, dve_s2_lo, i + 1)
                wait(pe, dve_x2, i)
                wait(pe, act_exp, 16 * i)
                for bank, w in ((0, 1), (1, 2), (2, 0)):
                    mm3(bank_a[bank][:], w_hi[:, w], w_lo[:, w], flat(s2_hi), flat(s2_lo),
                        True, True).then_inc(pe_proj, 1)
                wait(pe, act_x1, i + 1)
                wait(pe, dve_x1_lo, i + 1)
                mm3(bank_a[3][:], w_hi[:, 1], w_lo[:, 1], flat(x1_hi), flat(x1_lo), True, True).then_inc(pe_proj, 1)
                wait(pe, act_proj, 5 * i + 2)
                for b in range(NB):
                    last = nc.tensor.matmul(bank_a[1][:, b * P:b * P + P], x1[:, b], wraw[:, 2],
                                            start=True, stop=True)
                last.then_inc(pe_proj, 1)

            def self_(i, _):
                wait(pe, dve_q, 2 * i + 2)
                nc.tensor.matmul(bank_a[0][:], head_sum, flat(k_self), start=True, stop=True).then_inc(pe_self, 1)

            def S(i, n):
                b, g = divmod(n, G)
                if n == 0:
                    wait(pe, q_stacked, Q_DMAS * (i + 1))
                    wait(pe, k_stacked, K_DMAS * (i + 1))
                    wait(pe, act_self, i + 1)
                    wait(pe, act_proj, 5 * i + 5)
                if n >= 2:
                    wait(pe, dve_max, 16 * i + n - 1)
                for jj in range(J):
                    last = nc.tensor.matmul(bank_a[n % 2][:, jj * P:jj * P + P], qstack[0:96, g, b, jj],
                                            kstack[0:96, g, b], start=True, stop=True)
                last.then_inc(pe_s, 1)
                if b and g == 1:
                    turn_max(i, b - 1)

            def turn_max(i, b):
                wait(pe, dve_mexp, NB * i + b + 1)
                last = nc.tensor.transpose(bank_a[2][:, b * P:b * P + P],
                                           m_exp[:, b % 2].rearrange("p h d -> p (h d)"), ident)
                last.then_inc(pe_mt, 1)

            def mq(i, _):
                turn_max(i, NB - 1)

            def av(i, k):
                b, g = divmod(k, G)
                wait(pe, act_exp, 16 * i + k + 1)
                if g == 0:
                    wait(pe, pool_vpad, NB * i + b + 1)
                    if b == 0:
                        wait(pe, dve_mt, i + 1)
                for jj in range(J):
                    h = J * g + jj
                    half, hh = divmod(h, H // 2)
                    last = nc.tensor.matmul(attended(b, half), vpad[:, b % 2, h],
                                            probs[:, k % 2, jj], start=(hh == 0), stop=(hh == H // 2 - 1))
                last.then_inc(pe_av, 1)

            def E(i, k):
                b, g = divmod(k, G)
                if k == 0:
                    wait(pe, m_stacked, M_DMAS * (i + 1))
                    wait(pe, dve_max, 16 * (i + 1))
                if k >= 2:
                    wait(pe, act_exp, 16 * i + k - 1)
                nc.tensor.matmul(bank_a[k % 2][:], kstack[:, g, b],
                                 qstack[:, g, b].rearrange("p j t -> p (j t)"),
                                 start=True, stop=True).then_inc(pe_st, 1)
                if k:
                    av(i, k - 1)

            def Eend(i, _):
                av(i, NB * G - 1)

            def wo(i, _):
                wait(pe, pool_att, 2 * (i + 1))
                nc.tensor.matmul(bank_a[0][:], wraw[:, 3], flat(kf), start=True, stop=True).then_inc(pe_wo, 1)

            def f1(j, u):
                o, c = divmod(u, 4)
                layer, kind, e = OUTS[o]
                if u == 0:
                    wait(pe, act_x2, j + 1)
                    wait(pe, dve_x2_lo, j + 1)
                if u == L3_FIRST:
                    wait(pe, act_x3, j + 1)
                    wait(pe, dve_x3_lo, j + 1)
                wait(pe, act_unit, UNITS * j + u - 1)
                wait(pe, dve_lo, NSHARED * j + SHARED_BEFORE[u - 1] if u else NSHARED * j)
                bank = bank_h[u % 2]
                if kind == "shared":
                    last = mm3(bank[:], sh_hi[:, e, c * P:c * P + P], sh_lo[:, e, c * P:c * P + P],
                               flat(x2_hi), flat(x2_lo), True, True)
                else:
                    n = EXPERT_UNITS.index(u)
                    loads = 2 if n % RING < NE - RING else 1
                    wait(pe, ring_in[n % RING], 16 * (loads * j + n // RING + 1))
                    src = (x2 if layer == 2 else x3)[:, c]
                    for cc in range(FC):
                        last = nc.tensor.matmul(bank[:, cc * P:cc * P + P], ring[:, n % RING, cc * P:cc * P + P],
                                                src, start=True, stop=True)
                last.then_inc(pe_f1, 1)

            free_o = [(act_out, NO, 0), (dve_logit, 2, 0), (act_out, NO, 1), (act_out, NO, 3),
                      (dve_logit, 2, 1), (act_out, NO, 4), (act_out, NO, 5), (act_out, NO, 6)]
            slot_o = [0, 1, 0, 0, 1, 0, 1, 0]

            def f2(j, u):
                o, c = divmod(u, 4)
                _, kind, e = OUTS[o]
                bank = bank_o[slot_o[o]]
                if c == 0:
                    s, per, n = free_o[o]
                    wait(pe, s, per * j + n)
                wait(pe, act_unit, UNITS * j + u + 1)
                if kind == "shared":
                    wait(pe, dve_lo, NSHARED * j + SHARED_BEFORE[u + 1])
                    w = slice(F + c * P, F + c * P + P)
                    last = mm3(bank[:], sh_hi[:, e, w], sh_lo[:, e, w], h_hi[:, u % 2], h_lo[:, u % 2],
                               c == 0, c == FC - 1)
                else:
                    n = EXPERT_UNITS.index(u)
                    for cc in range(FC):
                        last = nc.tensor.matmul(bank[:, c * P:c * P + P],
                                                ring[:, n % RING, F + cc * P:F + cc * P + P], h_ex[:, u % 2, cc],
                                                start=(cc == 0), stop=(cc == FC - 1))
                last.then_inc(pe_f2, 1)

            def unit(j, u):
                f1(j, u)
                if u not in (0, L3_FIRST):
                    f2(j, u - 1)

            def l2end(j, _):
                f2(j, L3_FIRST - 1)

            def l3end(j, _):
                f2(j, UNITS - 1)

            def hid_(j, layer):
                if layer == 0:
                    wait(pe, act_out, NO * j + 3)
                    w, terms = g1_sb, MIX2
                else:
                    wait(pe, act_out, NO * j + 8)
                    wait(pe, dve_exmix, 2 * j + 2)
                    w, terms = gw1_sb, MIX3
                for n, o in enumerate(terms):
                    last = nc.tensor.matmul(bank_o[1][:, 0:NB], w[:, n], outs[:, o, :, 0],
                                            start=(n == 0), stop=(n == len(terms) - 1))
                last.then_inc(pe_hid, 1)

            def logit(j, layer):
                wait(pe, act_hid, 2 * j + layer + 1)
                for n in range(3 + layer):
                    last = nc.tensor.matmul(bank_o[1][:, 8 + NB * n:8 + NB * n + NB],
                                            (gw2_sb if layer else g2_sb)[:, n], hid[:, layer],
                                            start=True, stop=True)
                last.then_inc(pe_logit, 1)

            run({"lora1": lora1, "lora2": lora2, "proj": proj, "self": self_, "S": S, "mq": mq, "E": E,
                 "Eend": Eend, "wo": wo, "unit": unit, "l2end": l2end, "l3end": l3end, "hid": hid_,
                 "logit": logit}, pe)

        @block.scalar
        def _(act):
            def high(dst, src):
                return nc.scalar.activation(dst, src, ACT.Copy)

            act.wait_ge(consts_in, 16 * len(CONSTS))
            act.wait_ge(setup_gate, 1)
            nc.scalar.activation(gv[:], gv[:], ACT.Exp).then_inc(setup_gate_exp, 1)
            act.wait_ge(stage_in, 16 * NS)
            for e in range(NS):
                last = high(sh_hi[:, e], ring[:, e])
            last.then_inc(setup_act, 1)
            nc.scalar.activation(w_hi[:, 0], wraw[:, 0], ACT.Copy, scale=SCALE).then_inc(setup_act, 1)
            high(w_hi[:, 1:3], wraw[:, 1:3]).then_inc(setup_act, 1)
            nc.scalar.activation(kstack[96:128].rearrange("p g b t -> p (g b t)"),
                                 shift_row[96:128].broadcast_to([32, G * NB * P]), ACT.Copy).then_inc(setup_act, 1)

            def split_s(i, _):
                wait(act, s_in, 16 * (i + 1))
                wait(act, q_stacked, Q_DMAS * i)
                high(s2_hi[:], s2[:]).then_inc(act_s2, 1)

            def lora2(i, _):
                wait(act, dve_x1, i + 1)
                wait(act, k_stacked, K_DMAS * i)
                high(x1_hi[:], x1[:]).then_inc(act_x1, 1)

            def proj(i, _):
                wait(act, setup_dve, 2) if isinstance(i, int) and i == 0 else None
                wait(act, pool_att, 2 * i)
                wait(act, pe_proj, 5 * i + 1)
                nc.scalar.activation(flat(k_self), bank_a[0][:], ACT.Identity, bias=bias[:, 2:3]).then_inc(act_proj, 1)
                wait(act, pe_proj, 5 * i + 2)
                nc.scalar.activation(flat(v_self), bank_a[1][:], ACT.Copy).then_inc(act_proj, 1)
                wait(act, pe_proj, 5 * i + 3)
                wait(act, dve_s2_lo, i + 1)
                nc.scalar.activation(flat(s2_hi), bank_a[2][:], ACT.Identity, bias=bias[:, 0:1]).then_inc(act_proj, 1)
                wait(act, pe_proj, 5 * i + 4)
                wait(act, pe_wo, i)
                nc.scalar.activation(flat(kf), bank_a[3][:], ACT.Identity, bias=bias[:, 1:2]).then_inc(act_proj, 1)
                wait(act, pe_proj, 5 * i + 5)
                wait(act, pool_vpad, NB * i)
                nc.scalar.activation(flat(v_sb), bank_a[1][:], ACT.Copy).then_inc(act_proj, 1)
                wait(act, dve_kf, i + 1)
                high(x1_hi[:], kf[:]).then_inc(act_kh, 1)

            def self_(i, _):
                wait(act, pe_self, i + 1)
                wait(act, dve_s2_lo, i + 1)
                nc.scalar.activation(flat(s_self), bank_a[0][:], ACT.Copy).then_inc(act_self, 1)

            def E(i, k):
                wait(act, pe_st, 16 * i + k + 1)
                if k >= 2:
                    wait(act, pe_av, 16 * i + k - 1)
                nc.scalar.activation(probs[:, k % 2].rearrange("p j t -> p (j t)"), bank_a[k % 2][:],
                                     ACT.Exp).then_inc(act_exp, 1)

            def self_w(i, _):
                wait(act, dve_sub, i + 1)
                nc.scalar.activation(kf[:], kf[:], ACT.Exp).then_inc(act_ps, 1)

            def fin(i, pair):
                wait(act, pe_av, 16 * i + 8 * (pair + 1))
                lo, hi = slice(0, 64), slice(64, P)
                two = slice(2 * pair, 2 * pair + 2)
                sums = bank_a[2 + pair][:].rearrange("p (b h t) -> p b h t", b=2, h=2)
                for dst, rows_out, rows_in, half in ((k_self, lo, hi, 0), (k_self, hi, lo, 1),
                                                     (s_self, lo, lo, 0), (s_self, hi, hi, 1)):
                    nc.scalar.activation(dst[rows_out, two], sums[rows_in, :, half], ACT.Copy).then_inc(act_fin, 1)

            def split2(i, _):
                wait(act, dve_x2, i + 1)
                if not (isinstance(i, int) and i == 0):
                    wait(act, pe_f1, UNITS * (i - 1) + LAST_SPLIT)
                high(x2_hi[:], x2[:]).then_inc(act_x2, 1)

            def unit(j, u):
                wait(act, pe_f1, UNITS * j + u + 1)
                if u >= 2:
                    wait(act, pe_f2, UNITS * j + u - 1)
                elif not (isinstance(j, int) and j == 0):
                    wait(act, pe_f2, UNITS * j)
                kind = OUTS[u // 4][1]
                dst = h_hi[:, u % 2] if kind == "shared" else h_ex[:, u % 2].rearrange("p c t -> p (c t)")
                nc.scalar.activation(dst, bank_h[u % 2][:], ACT.Relu).then_inc(act_unit, 1)
                if u % 4 == 0 and u not in (0, L3_FIRST):
                    take(j, u // 4 - 1)

            slot_o = [0, 1, 0, 0, 1, 0, 1, 0]

            def take(j, o):
                wait(act, pe_f2, UNITS * j + 4 * o + 4)
                if o == 0:
                    wait(act, dve_exmix, 2 * j)
                if o == 1:
                    wait(act, dve_mix3, j)
                if o == 6:
                    wait(act, dve_mix2, j + 1)
                nc.scalar.activation(outs[:, TILE[o]].rearrange("p b t -> p (b t)"), bank_o[slot_o[o]][:],
                                     ACT.Copy).then_inc(act_out, 1)

            def l2end(j, _):
                take(j, 2)

            def l3end(j, _):
                take(j, 7)

            def hid_(j, layer):
                wait(act, pe_hid, 2 * j + layer + 1)
                nc.scalar.activation(hid[:, layer], bank_o[1][:, 0:NB], ACT.Relu).then_inc(act_hid, 1)

            def soft(j, layer):
                wait(act, dve_logit, 2 * j + layer + 1)
                n = 3 + layer
                nc.scalar.activation(gate[:, 0:n], gate[:, 0:n], ACT.Exp).then_inc(act_gate, 1)

            def mix2(j, _):
                wait(act, dve_mix2, j + 1)
                wait(act, pe_f1, UNITS * j + L3_FIRST)
                high(x2_hi[:], x3[:]).then_inc(act_x3, 1)

            run({"split_s": split_s, "lora2": lora2, "proj": proj, "self": self_, "E": E, "self_w": self_w, "fin": fin, "split2": split2,
                 "unit": unit, "l2end": l2end, "l3end": l3end, "hid": hid_, "soft": soft, "mix2": mix2}, act)

        @block.vector
        def _(dve):
            def low(dst, src, hi):
                return nc.vector.tensor_tensor(dst, src, hi.bitcast(F32), ALU.subtract)

            class Chain:
                def __init__(self, s):
                    self.s, self.n, self.base = s, 0, 0

                def __call__(self, ins):
                    ins.then_inc(self.s, 1)
                    self.n += 1

                def settle(self):
                    dve.wait_ge(self.s, self.base + self.n)

            c = Chain(setup_chain)
            dve.wait_ge(consts_in, 16 * len(CONSTS))
            c(nc.vector.tensor_copy(lens_f[:], ints[:, 0]))
            c(nc.vector.tensor_copy(labels_f[:], ints[:, 1]))
            c(nc.vector.tensor_copy(langs_f[:], ints[:, 2]))
            c(nc.vector.tensor_reduce(gv_s[:], gv[:], AXX, ALU.max))
            c.settle()
            c(nc.vector.tensor_scalar(key_mask[:], lens_f[:], part_no, None, ALU.is_gt))
            c(nc.vector.tensor_scalar(lang_hot[:], langs_f[:], lang_no, None, ALU.is_equal))
            c(nc.vector.tensor_tensor(gv[:], gv[:], gv_s[:].unsqueeze(2).broadcast_to([P, TYPES, 4]), ALU.subtract))
            c.settle()
            nc.vector.tensor_scalar(gv[:], gv[:], 10.0, None, ALU.mult).then_inc(setup_gate, 1)
            dve.wait_ge(setup_gate_exp, 1)
            c(nc.vector.tensor_reduce(gv_s[:], gv[:], AXX, ALU.add))
            c.settle()
            c(nc.vector.reciprocal(gv_s[:], gv_s[:]))
            c.settle()
            c(nc.vector.tensor_tensor(gv[:], gv[:], gv_s[:].unsqueeze(2).broadcast_to([P, TYPES, 4]), ALU.mult))
            c.settle()
            for k in range(2):
                c(nc.vector.tensor_scalar(wab[:, k], labels_f[:], 0.0, gv[:, 0, k:k + 1], ALU.is_equal, ALU.mult))
                for t in range(1, TYPES):
                    c(nc.vector.tensor_scalar(wab_t, labels_f[:], float(t), gv[:, t, t + k:t + k + 1],
                                              ALU.is_equal, ALU.mult))
                    c.settle()
                    c(nc.vector.tensor_tensor(wab[:, k], wab[:, k], wab_t, ALU.add))
                    c.settle()
            dve.wait_ge(setup_act, 1)
            for e in range(NS):
                last = low(sh_lo[:, e], ring[:, e], sh_hi[:, e])
            last.then_inc(setup_dve, 1)
            dve.wait_ge(setup_act, 3)
            nc.vector.scalar_tensor_tensor(w_lo[:, 0], wraw[:, 0], SCALE, w_hi[:, 0].bitcast(F32), ALU.mult,
                                           ALU.subtract)
            low(w_lo[:, 1:3], wraw[:, 1:3], w_hi[:, 1:3])
            dve.wait_ge(setup_pe, 1)
            c(nc.vector.tensor_scalar(bias[:, 0:1], bank_a[0][:, 0:1], vec[:, 0:1], SCALE, ALU.add, ALU.mult))
            c(nc.vector.tensor_scalar(bias[:, 1:3], bank_a[0][:, 1:3], vec[:, 1:2], None, ALU.add))
            c(nc.vector.tensor_scalar(bias[:, 3:4], bank_a[0][:, 3:4], vec[:, 3:4], None, ALU.add))
            c.settle()
            nc.vector.tensor_copy(bq_s[:], bias[:, 0:1]).then_inc(setup_dve, 1)
            dve.wait_ge(setup_dve, 2)

            def lora1(i, _):
                at = bass.ds(i * NB, NB)
                wait(dve, pool_vpad, NB * i)
                wait(dve, pe_lora, 2 * i)
                nc.vector.tensor_copy(hot_g[:], lang_hot[:, at]).then_inc(dve_tables, 1)
                nc.vector.tensor_copy(mask_g[:], key_mask[:, at]).then_inc(dve_pre, 1)
                nc.vector.tensor_copy(len_g[:], lens_f[:, at]).then_inc(dve_tables, 1)
                dve.wait_ge(dve_tables, 4 * i + 2)
                nc.vector.tensor_tensor(pad_key[:], key_no.unsqueeze(1).broadcast_to([P, NB, P]),
                                        per_key(len_g[:]), ALU.is_ge).then_inc(dve_tables, 1)
                nc.vector.tensor_copy(adapt[LR:LR + LANGS],
                                      per_key(hot_g[LR:LR + LANGS], LANGS)).then_inc(dve_adapt, 1)
                wait(dve, pe_lora, 2 * i + 1)
                nc.vector.tensor_tensor(adapt[0:LR], bank_a[2][0:LR].rearrange("p (b t) -> p b t", b=NB),
                                        per_key(hot_g[0:LR], LR), ALU.mult).then_inc(dve_adapt, 1)

            def split_s(i, _):
                wait(dve, act_s2, i + 1)
                wait(dve, q_stacked, Q_DMAS * i)
                low(s2_lo[:], s2[:], s2_hi[:]).then_inc(dve_s2_lo, 1)

            def lora2(i, _):
                wait(dve, dve_x2, i)
                wait(dve, pe_lora, 2 * i + 2)
                nc.vector.tensor_tensor(flat(x1), flat(x0), bank_a[3][:], ALU.add).then_inc(dve_x1, 1)
                wait(dve, act_x1, i + 1)
                wait(dve, k_stacked, K_DMAS * i)
                low(x1_lo[:], x1[:], x1_hi[:]).then_inc(dve_x1_lo, 1)

            def proj(i, _):
                wait(dve, act_proj, 5 * i + 3)
                nc.vector.scalar_tensor_tensor(flat(s2_lo), bank_a[2][:], bq_s[:, 0:1], flat(s2_hi).bitcast(F32),
                                               ALU.add, ALU.subtract).then_inc(dve_q, 1)
                wait(dve, act_proj, 5 * i + 4)
                nc.vector.tensor_copy(k_first[:], kf[:, :, 0]).then_inc(dve_tables, 1)
                dve.wait_ge(dve_tables, 4 * i + 4)
                nc.vector.scalar_tensor_tensor(flat(k_self), bank_a[2][:], bq_s[:, 0:1], flat(k_self),
                                               ALU.add, ALU.mult).then_inc(dve_q, 1)
                for b in range(NB):
                    last = nc.vector.copy_predicated(kf[:, b], pad_key[:, b], k_first[:, b:b + 1].broadcast_to([P, P]))
                last.then_inc(dve_kf, 1)
                wait(dve, act_kh, i + 1)
                low(x1_lo[:], kf[:], x1_hi[:]).then_inc(dve_k_lo, 1)

            def S(i, n):
                b, g = divmod(n, G)
                wait(dve, pe_s, 16 * i + n + 1)
                nc.vector.tensor_reduce(m_nat[:, b, J * g:J * g + J],
                                        bank_a[n % 2][:].rearrange("p (j t) -> p j t", j=J),
                                        AXX, ALU.max).then_inc(dve_max, 1)
                if g < G - 1:
                    return
                dve.wait_ge(dve_max, 16 * i + n + 1)
                if b >= 2:
                    wait(dve, pe_mt, NB * i + b - 1)
                nc.vector.tensor_copy(m_exp[:, b % 2],
                                      m_nat[:, b].unsqueeze(2).broadcast_to([P, H, DH])).then_inc(dve_mexp, 1)

            def mq(i, _):
                wait(dve, pe_mt, NB * (i + 1))
                wait(dve, act_self, i + 1)
                wait(dve, m_stacked, M_DMAS * i)
                nc.vector.tensor_tensor(flat(mt), bank_a[2][:], flat(s_self), ALU.max).then_inc(dve_mt, 1)

            def self_w(i, _):
                dve.wait_ge(dve_mt, i + 1)
                dve.wait_ge(dve_k_lo, i + 1)
                nc.vector.tensor_tensor(kf[:], s_self[:], mt[:].bitcast(F32), ALU.subtract).then_inc(dve_sub, 1)

            def rec(i, b):
                wait(dve, pool_den, 2 * i + b // 2 + 1)
                nc.vector.reciprocal(k_self[:, b], k_self[:, b]).then_inc(dve_rec, 1)

            def wo(i, _):
                wait(dve, pe_wo, i + 1)
                if not (isinstance(i, int) and i == 0):
                    wait(dve, pe_f1, UNITS * (i - 1) + X2_EXPERTS)
                nc.vector.scalar_tensor_tensor(flat(x2), bank_a[0][:], bias[:, 3:4], flat(x1),
                                               ALU.add, ALU.add).then_inc(dve_x2, 1)

            def split2(i, _):
                wait(dve, act_x2, i + 1)
                low(x2_lo[:], x2[:], x2_hi[:]).then_inc(dve_x2_lo, 1)

            def unit(j, u):
                if OUTS[u // 4][1] == "shared":
                    wait(dve, act_unit, UNITS * j + u + 1)
                    nc.vector.scalar_tensor_tensor(h_lo[:, u % 2], bank_h[u % 2][:], 0.0,
                                                   h_hi[:, u % 2].bitcast(F32), ALU.max,
                                                   ALU.subtract).then_inc(dve_lo, 1)

            def logit(j, layer):
                wait(dve, pe_logit, 2 * j + layer + 1)
                n = 3 + layer
                lg = bank_o[1][:, 8:8 + NB * n].rearrange("p (w b) -> p w b", b=NB)
                nc.vector.tensor_reduce(gmax[:], lg.rearrange("p w b -> p b w"), AXX, ALU.max).then_inc(dve_gate, 1)
                dve.wait_ge(dve_gate, 8 * j + 4 * layer + 1)
                nc.vector.tensor_tensor(gate[:, 0:n], lg, gmax[:].unsqueeze(1).broadcast_to([P, n, NB]),
                                        ALU.subtract).then_inc(dve_logit, 1)

            def soft(j, layer):
                wait(dve, act_gate, 2 * j + layer + 1)
                n = 3 + layer
                base = 8 * j + 4 * layer
                nc.vector.tensor_reduce(gmax[:], gate[:, 0:n].rearrange("p w b -> p b w"), AXX,
                                        ALU.add).then_inc(dve_gate, 1)
                dve.wait_ge(dve_gate, base + 2)
                nc.vector.reciprocal(gmax[:], gmax[:]).then_inc(dve_gate, 1)
                dve.wait_ge(dve_gate, base + 3)
                nc.vector.tensor_tensor(gate[:, 0:n], gate[:, 0:n], gmax[:].unsqueeze(1).broadcast_to([P, n, NB]),
                                        ALU.mult).then_inc(dve_gate, 1)
                dve.wait_ge(dve_gate, base + 4)

            def add_term(dst, o, weight, acc, b, s):
                nc.vector.scalar_tensor_tensor(dst[:, b], outs[:, o, b], weight, acc[:, b],
                                               ALU.mult, ALU.add).then_inc(s, 1)

            def mix2(j, _):
                wait(dve, stored, 16 * j)
                wait(dve, act_out, NO * j + 3)
                for n in range(3):
                    for b in range(NB):
                        last_term = n == 2 and b == NB - 1
                        if n:
                            dve.wait_ge(dve_term, 24 * j + NB * (n - 1) + b + 1)
                        add_term(x3, MIX2[n], gate[:, n, b:b + 1], x3 if n else x2, b, dve_term)
                dve.wait_ge(dve_term, 24 * j + 12)
                nc.vector.tensor_copy(wab_g[:], wab[:, :, bass.ds(j * NB, NB)]).then_inc(dve_mix2, 1)
                wait(dve, act_x3, j + 1)
                low(x2_lo[:], x3[:], x2_hi[:]).then_inc(dve_x3_lo, 1)

            def exmix(j, _):
                wait(dve, act_out, NO * j + 8)
                dve.wait_ge(dve_mix2, j + 1)
                for b in range(NB):
                    last = nc.vector.tensor_scalar(outs[:, TILE[6], b], outs[:, TILE[6], b], wab_g[:, 0, b:b + 1], None, ALU.mult)
                last.then_inc(dve_exmix, 1)
                dve.wait_ge(dve_exmix, 2 * j + 1)
                for b in range(NB):
                    last = nc.vector.scalar_tensor_tensor(outs[:, TILE[6], b], outs[:, TILE[7], b], wab_g[:, 1, b:b + 1],
                                                          outs[:, TILE[6], b], ALU.mult, ALU.add)
                last.then_inc(dve_exmix, 1)

            def mix3(j, n):
                if n == 0:
                    dve.wait_ge(dve_exmix, 2 * j + 2)
                    wait(dve, pe_f1, UNITS * j + UNITS)
                for b in range(NB):
                    if n:
                        dve.wait_ge(dve_term, 24 * j + 12 + NB * (n - 1) + b + 1)
                    ins = nc.vector.scalar_tensor_tensor(x3[:, b], outs[:, MIX3[n], b], gate[:, n, b:b + 1],
                                                         x3[:, b], ALU.mult, ALU.add)
                    if n < 3:
                        ins.then_inc(dve_term, 1)
                if n == 3:
                    ins.then_inc(dve_mix3, 1)

            run({"lora1": lora1, "split_s": split_s, "lora2": lora2, "proj": proj, "S": S, "mq": mq, "self_w": self_w, "rec": rec, "wo": wo, "split2": split2,
                 "unit": unit, "logit": logit, "soft": soft, "mix2": mix2, "exmix": exmix, "mix3": mix3}, dve)


def kernel(x, itok_B_0_3, fside_BxSxS_0, itok_B_18_1004, itok_B_0_2, L0_cond_lora_A, L0_cond_lora_B,
           L0_cond_lang_embed, L1_cond_Wq, L1_cond_bq, L1_cond_Wk, L1_cond_bk, L1_cond_Wv, L1_cond_bv,
           L1_cond_Wo, L1_cond_bo, L1_cond_b_prev, L1_cond_b_self, L2_cond_wi, L2_cond_wo, L2_cond_swi,
           L2_cond_swo, L2_cond_g1, L2_cond_g2, L3_cond_expert_wi, L3_cond_expert_wo, L3_cond_share_wi,
           L3_cond_share_wo, L3_cond_gate_vecs, L3_cond_gate_w1, L3_cond_gate_w2):
    import concourse.bacc as bacc
    from concourse.bass_utils import run_bass_kernel_spmd

    a = np.asarray
    B = a(x).shape[0]
    groups = B // NB

    def turned(t):
        return np.ascontiguousarray(a(t).reshape(groups, NB, P, P).transpose(0, 3, 1, 2))

    def rows(t):
        return np.ascontiguousarray(np.broadcast_to(a(t).reshape(1, -1), (P, a(t).size)))

    def expert(wi, wo):
        wi, wo = a(wi), a(wo)
        n = wi.shape[0]
        wo = wo.reshape(n, FC, P, P).transpose(0, 2, 1, 3).reshape(n, P, FC * P)
        return np.ascontiguousarray(np.concatenate([wi, wo], axis=2))

    def cut(w, n):
        return np.ascontiguousarray(a(w).reshape(n, P, P).transpose(1, 0, 2))

    def spread(w):
        return np.ascontiguousarray(np.broadcast_to(a(w)[:, :, None], (P, a(w).shape[1], P)))

    p = np.arange(P)
    consts = np.zeros((P, 3 * P + 3), np.float32)
    consts[:, 0:P] = np.eye(P)
    consts[:, P:2 * P] = (p[:, None] // DH == p[None, :] // DH)
    consts[:, 2 * P:3 * P] = p[None, :]
    consts[:, 3 * P] = p
    consts[:, 3 * P + 1] = np.where(p < LR, p // RANK, p - LR)
    consts[:, 3 * P + 2] = np.where((p >= 96) & (p % DH == 0), -1, 0)

    shared = np.concatenate([expert(L2_cond_swi, L2_cond_swo), expert(L3_cond_share_wi, L3_cond_share_wo)])
    loraB = a(L0_cond_lora_B).transpose(0, 2, 1).reshape(LR, P)
    arrays = {
        "xT": turned(x), "sT": turned(fside_BxSxS_0),
        "lens": rows(itok_B_18_1004), "labels": rows(itok_B_0_2), "langs": rows(itok_B_0_3),
        "loraA": np.ascontiguousarray(a(L0_cond_lora_A).reshape(LR, P).T),
        "loraBe": np.concatenate([loraB, a(L0_cond_lang_embed)]),
        "wqkvo": np.ascontiguousarray(np.stack([a(L1_cond_Wq), a(L1_cond_Wk), a(L1_cond_Wv), a(L1_cond_Wo)], 1)),
        "vecs": np.ascontiguousarray(np.stack([a(v).reshape(P) for v in (
            L1_cond_bq, L1_cond_bk, L1_cond_bv, L1_cond_bo, L1_cond_b_prev, L1_cond_b_self)], 1)),
        "shared": np.ascontiguousarray(shared.transpose(1, 0, 2)),
        "experts2": expert(L2_cond_wi, L2_cond_wo), "experts3": expert(L3_cond_expert_wi, L3_cond_expert_wo),
        "g1": cut(L2_cond_g1, 3), "g2r": spread(L2_cond_g2),
        "gw1": cut(L3_cond_gate_w1, 4), "gw2r": spread(L3_cond_gate_w2),
        "gate_vecs": rows(L3_cond_gate_vecs).reshape(P, TYPES, 4),
        "consts": consts,
    }
    nc = bacc.Bacc("TRN2", target_bir_lowering=False, num_devices=1)
    args = [nc.dram_tensor(n, v.shape, mybir.dt.from_np(v.dtype), kind="ExternalInput").ap()
            for n, v in arrays.items()]
    out = nc.dram_tensor("out", (groups, P, NB, P), F32, kind="ExternalOutput").ap()
    parts = [nc.dram_tensor(n, s, F32, kind="Internal").ap()
             for n, s in (("q_parts", (2, P // G, G, NB, P)), ("k_parts", (2, P // G, G, NB, P)),
                          ("m_parts", (P // G, G, NB, P)))]
    cond_resid_kernel(nc, *args, *parts, out)
    r = run_bass_kernel_spmd(nc, [arrays], core_ids=[0])
    got = r.results[0]["out"]
    return np.ascontiguousarray(np.asarray(got).transpose(0, 2, 3, 1).reshape(B, P, P))
```

```python
from contextlib import ExitStack

import numpy as np

import concourse.bass as bass
from concourse import mybir

ALU = mybir.AluOpType
ACT = mybir.ActivationFunctionType
AXX = mybir.AxisListType.X
F32 = mybir.dt.float32
F32R = mybir.dt.float32r
I32 = mybir.dt.int32
U8 = mybir.dt.uint8

P = 128
NB = 4
H = 16
DH = P // H
G = 4
J = H // G
PARTS = 3
STACKED = PARTS * J * DH
FC = 4
LANGS, RANK = 4, 16
LR = LANGS * RANK
TYPES = 3
SCALE = float(np.float32(1.0) / np.sqrt(np.float32(DH)))
RING = 6

OUTS = [(2, "expert", 0), (2, "shared", 0), (2, "shared", 1),
        (3, "expert", 1), (3, "expert", 2), (3, "shared", 2), (3, "shared", 3), (3, "shared", 4)]
TILE = (0, 1, 2, 3, 0, 1, 4, 5)
MIX2 = (0, 1, 2)
MIX3 = (3, 1, 4, 5)
ADD3 = (1, 0, 2, 3)
UNITS = 4 * len(OUTS)
L3_FIRST = 12
NO = len(OUTS)
EXPERT_UNITS = [4 * o + b for o, (_, kind, _) in enumerate(OUTS) if kind == "expert" for b in range(NB)]
NE = len(EXPERT_UNITS)
SHARED_BEFORE = [sum(OUTS[v // 4][1] == "shared" for v in range(u)) for u in range(UNITS + 1)]
NSHARED = SHARED_BEFORE[UNITS]
SHARED2_FIRST = min(u for u in range(UNITS) if OUTS[u // 4][1] == "shared")
SHARED3_FIRST = min(u for u in range(L3_FIRST, UNITS) if OUTS[u // 4][1] == "shared")
X3_EXPERTS = max(EXPERT_UNITS) + 1


def p(name, k=0):
    return 1, name, k


def a(name, k=0):
    return 0, name, k


def f(name, k=0):
    return -1, name, k


def l(name, k=0):
    return -2, name, k


def among_units(steps_at):
    steps = []
    for u in range(UNITS):
        steps.append(f("f1", u))
        if u == L3_FIRST - 1:
            steps += [f("f2", u - 1), f("f2", u)]
        steps += steps_at.get(u, [])
        if u not in (0, L3_FIRST - 1, L3_FIRST):
            steps.append(f("f2", u - 1))
        steps += steps_at.get(u + 0.5, [])
    return steps + [f("f2", UNITS - 1)]


def numbered(name, n):
    if name == "S" and n >= G and n % G == 1:
        return [a("mexp", n // G - 1), a(name, n)]
    return [a(name, n)]


def spread(name, places):
    at, n = {}, 0
    for u, count in places:
        at[u] = [step for m in range(n, n + count) for step in numbered(name, m)]
        n += count
    assert n == NB * G
    return at


def join(*maps):
    return {u / 2: [s for m in maps for s in m.get(u / 2, [])] for u in range(2 * UNITS)}


START = [a("load"), a("consts"), a("load_s"), a("stage"), a("lora1"), a("biases"), a("split_s"),
         a("lora2"), a("proj"), a("self"), a("stack"), a("weights"), p("load"),
         *[step for n in range(NB * G) for step in numbered("S", n)], a("mexp", NB - 1), a("mq"),
         a("self_sub"), a("self_w"), a("E", 0), a("E", 1), a("split_w", 0), a("E", 2), a("E", 3),
         a("split_w", 1), a("E", 4), a("E", 5), a("split_w", 2), a("E", 6), a("E", 7), a("split_w", 3),
         a("E", 8), a("E", 9), a("fin", 0), a("split_w", 4), a("E", 10), a("E", 11), a("rec", 0), a("rec", 1),
         a("E", 12), a("E", 13), a("att", 0), a("E", 14), a("E", 15), a("Eend"), a("fin", 1),
         a("rec", 2), a("rec", 3), a("att", 1), p("load_s"), a("wo"), p("lora1")]
SECOND = among_units(join(
    spread("S", [(9, 1), (9.5, 1), (10, 1), (10.5, 2), (11, 2), (12, 2), (12.5, 1), (13, 2), (13.5, 1),
                 (14, 2), (14.5, 1)]),
    spread("E", [(19, 5), (20, 5), (21, 6)]),
    {0: [a("lora2"), a("split_s"), f("split2")], 1: [a("proj"), a("stack"), p("load")], 2: [a("self")],
     11: [f("hid", 0), f("logit", 0), f("soft", 0), f("mix2")], 14: [f("split3")],
     15: [a("mexp", NB - 1)], 15.5: [a("mq"), a("self_sub")], 17: [a("self_w")], 20.5: [a("fin", 0)],
     21.5: [a("rec", 0), a("rec", 1), a("Eend")], 22.5: [a("fin", 1), a("att", 0)],
     23.5: [a("rec", 2), a("rec", 3), a("att", 1), p("load_s"), p("lora1")], 24: [f("exmix")], 24.5: [a("wo")],
     25.5: [p("lora2"), p("split_s")], 26.5: [p("proj"), p("stack")], 27.5: [p("self")]}))
STEADY = among_units(join(
    spread("S", [(0, 2), (1, 2), (1.5, 2), (2, 1), (2.5, 2), (3, 1), (3.5, 2), (4, 1), (4.5, 1), (5, 1), (5.5, 1)]),
    {0: [f("split2")], 1.5: [l("hid", 1)], 2.5: [l("logit", 1)], 3: [l("soft", 1)], 4: [l("mix3", 0)],
     5: [l("mix3", 1)], 6: [a("mexp", NB - 1), l("mix3", 2)],
     7: [a("mq"), l("mix3", 3), a("self_sub")],
     11: [a("E", 0), f("hid", 0), a("E", 1), f("logit", 0), a("E", 2), f("soft", 0), a("E", 3),
          f("mix2"), a("E", 4), a("E", 5)],
     12: [a("E", 6), a("self_w"), p("load")], 12.5: [a("E", 7)], 13: [a("E", 8), f("split3")], 13.5: [a("E", 9)],
     14: [a("E", 10), a("fin", 0)], 14.5: [a("E", 11)], 15: [a("E", 12), a("rec", 0), a("rec", 1)], 15.5: [a("E", 13)],
     16: [a("E", 14), a("att", 0)], 16.5: [a("E", 15)], 17: [a("Eend"), a("fin", 1)], 18: [a("rec", 2), a("rec", 3)],
     19: [a("att", 1), p("load_s"), p("lora1")], 20: [a("wo")], 21: [p("lora2"), p("split_s"), f("exmix")],
     23: [p("proj")], 24: [p("stack")], 25: [p("self")]}))
END = [l("hid", 1), l("logit", 1), l("soft", 1), *[l("last_mix3", n) for n in range(4)]]


def cond_resid_kernel(nc, xT, sT, lens, labels, langs, loraA, loraBe, wqkvo, vecs, shared, experts2,
                      experts3, g1, g2r, gw1, gw2r, gate_vecs, consts, q_parts, k_parts, out):
    groups = xT.shape[0]
    NSEQ = groups * NB
    NS = shared.shape[1]
    FW = shared.shape[2]
    F = FC * P
    experts = [experts2, experts3, experts3]

    with ExitStack() as ctx:
        def sb(name, shape, dt=F32):
            return ctx.enter_context(nc.sbuf_tensor(name, shape, dt))

        def ps(name, shape):
            return ctx.enter_context(nc.psum_tensor(name, shape, F32))

        def sem(name):
            return ctx.enter_context(nc.semaphore(name))

        bank_a = [ps(f"bank_a{k}", [P, 512]) for k in range(4)]
        bank_h = [ps(f"bank_h{k}", [P, 512]) for k in range(2)]
        bank_o = [ps(f"bank_o{k}", [P, 512]) for k in range(2)]

        ring = sb("ring", [P, RING, FW])
        sh_hi = sb("sh_hi", [P, NS, FW], F32R)
        sh_lo = sb("sh_lo", [P, NS, FW], F32R)
        wraw = sb("wraw", [P, 4, P])
        w_hi = sb("w_hi", [P, 3, P], F32R)
        w_lo = sb("w_lo", [P, 3, P], F32R)
        lora_a = sb("lora_a", [P, LR])
        lora_be = sb("lora_be", [LR + LANGS, P])
        g1_sb = sb("g1_sb", [P, 3, P])
        g2_sb = sb("g2_sb", [P, 3])
        gw1_sb = sb("gw1_sb", [P, 4, P])
        gw2_sb = sb("gw2_sb", [P, 4])
        vec = sb("vec", [P, 6])
        bias = sb("bias", [P, 4])
        bq_s = sb("bq_s", [P, 1])
        const = sb("const", [P, 4 * P + 3])
        ident = const[:, 0:P]
        head_sum = const[:, P:2 * P]
        key_no = const[:, 2 * P:3 * P]
        all_sum = const[:, 3 * P:4 * P]
        part_no = const[:, 4 * P:4 * P + 1]
        lang_no = const[:, 4 * P + 1:4 * P + 2]
        shift_row = const[:, 4 * P + 2:4 * P + 3]

        ints = sb("ints", [P, 3, NSEQ], I32)
        lens_f = sb("lens_f", [P, NSEQ])
        labels_f = sb("labels_f", [P, NSEQ])
        langs_f = sb("langs_f", [P, NSEQ])
        key_mask = sb("key_mask", [P, NSEQ])
        lang_hot = sb("lang_hot", [P, NSEQ])
        gv = sb("gv", [P, TYPES, 4])
        gv_s = sb("gv_s", [P, TYPES])
        wab = sb("wab", [P, 2, NSEQ])

        x0 = sb("x0", [P, NB, P])
        x1 = sb("x1", [P, NB, P])
        s2 = sb("s2", [P, NB, P])
        x1_hi = sb("x1_hi", [P, NB, P], F32R)
        x1_lo = sb("x1_lo", [P, NB, P], F32R)
        s2_hi = sb("s2_hi", [P, NB, P], F32R)
        s2_lo = sb("s2_lo", [P, NB, P], F32R)
        adapt = sb("adapt", [LR + LANGS, NB, P])
        hot_g = sb("hot_g", [P, NB])
        len_g = sb("len_g", [P, NB])
        mask_g = sb("mask_g", [P, NB])
        wab_g = sb("wab_g", [P, 2, NB])
        pad_key = sb("pad_key", [P, NB, P], U8)
        kf = sb("kf", [P, NB, P])
        k_first = sb("k_first", [P, NB])
        k_self = sb("k_self", [P, NB, P])
        v_self = sb("v_self", [P, NB, P])
        s_self = s2
        v_sb = sb("v_sb", [P, NB, P])
        padded = sb("padded", [P, G, NB, J, P], F32R)
        qstack = sb("qstack", [STACKED, G, NB, P], F32R)
        kstack = sb("kstack", [P, G, NB, P], F32R)
        vpad = sb("vpad", [P, 2, H, P])
        m_nat = sb("m_nat", [P, NB, H])
        m_exp = sb("m_exp", [P, 2, H, DH])
        mt = sb("mt", [P, NB, P], F32R)
        probs = sb("probs", [P, 2, J, P])
        x2 = sb("x2", [P, NB, P])
        wab_t = x2[:, 0, 0:NSEQ]

        x3 = sb("x3", [P, NB, P])
        x2_hi = sb("x2_hi", [P, NB, P], F32R)
        x2_lo = sb("x2_lo", [P, NB, P], F32R)
        h_hi = sb("h_hi", [P, 2, 512], F32R)
        h_lo = sb("h_lo", [P, 2, 512], F32R)
        h_ex = sb("h_ex", [P, 2, FC, P])
        outs = sb("outs", [P, max(TILE) + 1, NB, P])
        weighed = sb("weighed", [P, 4, NB])
        gate = sb("gate", [P, 4, NB])
        gmax = sb("gmax", [P, NB])

        consts_in = sem("consts_in")
        late_in = sem("late_in")
        stage_in = sem("stage_in")
        x_in = sem("x_in")
        s_in = sem("s_in")
        ring_in = [sem(f"ring_in{k}") for k in range(RING)]
        q_saved = sem("q_saved")
        k_saved = sem("k_saved")
        k_padded = sem("k_padded")
        q_padded = sem("q_padded")
        q_stacked = sem("q_stacked")
        k_stacked = sem("k_stacked")
        m_stacked = sem("m_stacked")
        stored = sem("stored")
        setup_dve = sem("setup_dve")
        setup_act = sem("setup_act")
        setup_pe = sem("setup_pe")
        setup_pool = sem("setup_pool")
        setup_gate = sem("setup_gate")
        setup_gate_exp = sem("setup_gate_exp")
        setup_chain = sem("setup_chain")
        pe_lora = sem("pe_lora")
        pe_proj = sem("pe_proj")
        pe_self = sem("pe_self")
        pe_s = sem("pe_s")
        pe_mt = sem("pe_mt")
        pe_st = sem("pe_st")
        pe_av = sem("pe_av")
        pe_wo = sem("pe_wo")
        pe_f1 = sem("pe_f1")
        pe_f2 = sem("pe_f2")
        pe_hid = sem("pe_hid")
        pe_logit = sem("pe_logit")
        act_s2 = sem("act_s2")
        act_x1 = sem("act_x1")
        act_proj = sem("act_proj")
        act_kh = sem("act_kh")
        act_mexp = sem("act_mexp")
        act_self = sem("act_self")
        act_exp = sem("act_exp")
        act_ps = sem("act_ps")
        act_fin = sem("act_fin")
        act_x2 = sem("act_x2")
        act_x3 = sem("act_x3")
        act_unit = sem("act_unit")
        act_out = sem("act_out")
        act_gate = sem("act_gate")
        dve_adapt = sem("dve_adapt")
        dve_x1 = sem("dve_x1")
        dve_x1_lo = sem("dve_x1_lo")
        dve_s2_lo = sem("dve_s2_lo")
        dve_q = sem("dve_q")
        dve_kf = sem("dve_kf")
        dve_k_lo = sem("dve_k_lo")
        dve_max = sem("dve_max")
        dve_mt = sem("dve_mt")
        dve_pre = sem("dve_pre")
        dve_rec = sem("dve_rec")
        dve_x2 = sem("dve_x2")
        dve_lo = sem("dve_lo")
        dve_hid = sem("dve_hid")
        dve_logit = sem("dve_logit")
        dve_mix2 = sem("dve_mix2")
        dve_x3_lo = sem("dve_x3_lo")
        dve_tables = sem("dve_tables")
        dve_gate = sem("dve_gate")
        dve_term = sem("dve_term")
        pool_vpad = sem("pool_vpad")
        pool_sub = sem("pool_sub")
        pool_pv = sem("pool_pv")
        pool_x2_lo = sem("pool_x2_lo")
        pool_exmix = sem("pool_exmix")
        pool_term = sem("pool_term")
        mixed3 = sem("mixed3")
        pool_den = sem("pool_den")
        pool_num = sem("pool_num")
        pool_att = sem("pool_att")

        CONSTS = [(lora_a[:], loraA), (const[:], consts), (ints[:, 2], langs), (ints[:, 0], lens),
                  (ints[:, 1], labels), (lora_be[:], loraBe), (wraw[:], wqkvo), (vec[:], vecs)]
        LATE_CONSTS = [(gv[:], gate_vecs), (g1_sb[:], g1), (g2_sb[:], g2r), (gw1_sb[:], gw1), (gw2_sb[:], gw2r)]

        def attended(b, half):
            c = (2 * (b % 2) + half) * P
            return bank_a[2 + b // 2][:, c:c + P]

        slot_o = [0, 1, 0, 0, 1, 0, 1, 0]
        SAVES, STACKS, PADS = PARTS * 16, 16, J * 16

        def wait(eng, s, value):
            if isinstance(value, int) and value <= 0:
                return
            eng.wait_ge(s, value)

        def flat(tile):
            return tile[:].rearrange("p b t -> p (b t)")

        def mixed(n, b):
            return 6 * (b // 2) + 2 * n + b % 2 + 1

        def per_key(ap, parts=P):
            return ap.unsqueeze(2).broadcast_to([parts, NB, P])

        def walk(handlers, schedule, t):
            for ahead, name, k in schedule:
                if name in handlers and (not isinstance(t, int) or 0 <= t + ahead < groups):
                    handlers[name](t + ahead, k)

        def run(handlers, engine):
            last = groups - 1
            walk(handlers, START, 0)
            walk(handlers, SECOND, 1)
            with engine.Fori(2, last) as t:
                walk(handlers, STEADY, t)
            walk(handlers, STEADY, last)
            walk(handlers, STEADY, last + 1)
            walk(handlers, END, last + 2)

        block = ctx.enter_context(nc.Block())

        @block.sync
        def _(sp):
            def constants(i, _):
                for dst, src in CONSTS:
                    sp.dma_start(dst, src).then_inc(consts_in, 16)

            def stage(i, _):
                for dst, src in LATE_CONSTS:
                    sp.dma_start(dst, src).then_inc(late_in, 16)
                for e in range(NS):
                    sp.dma_start(ring[:, e], shared[:, e]).then_inc(stage_in, 16)

            def split_w(i, e):
                sp.wait_ge(consts_in, 16 * len(CONSTS))
                sp.wait_ge(setup_dve, 2 + e)
                for n in range(e, RING if e == NS - 1 else e + 1):
                    fetch(0, n)

            def wait_first(s, value):
                wait(sp, s, value)
                if not isinstance(value, int):
                    sp.wait_ge(consts_in, 16 * len(CONSTS))

            def fetch(group, n, s=None, value=None):
                which, b = divmod(n, NB)
                label = sp.value_load(ints[0:1, 1, bass.ds(group * NB + b, 1)], min_val=0, max_val=TYPES - 1)
                if which == 2:
                    label = label + 1
                src = experts[which][bass.ds(label, 1)].rearrange("o p f -> (o p) f")
                if s is not None:
                    wait_first(s, value)
                sp.dma_start(ring[:, n % RING], src).then_inc(ring_in[n % RING], 16)

            def load(i, _):
                wait_first(dve_x1, i)
                sp.dma_start(x0[:], xT[bass.ds(i, 1)].rearrange("o p b t -> (o p) b t")).then_inc(x_in, 16)

            def load_s(i, _):
                wait_first(pool_att, 2 * i)
                sp.dma_start(s2[:], sT[bass.ds(i, 1)].rearrange("o p b t -> (o p) b t")).then_inc(s_in, 16)

            def refill(j, u):
                done = u - 2
                if done in EXPERT_UNITS:
                    n = EXPERT_UNITS.index(done)
                    last = isinstance(j, int) and j == groups - 1
                    if n < NE - RING:
                        fetch(j, n + RING, pe_f2, UNITS * j + done + 1)
                    elif not last:
                        fetch(j + 1, n if n < RING else n - RING, pe_f2, UNITS * j + done + 1)

            def mix3(j, n):
                if n < 3:
                    return
                wait_first(mixed3, 4 * (j + 1))
                sp.dma_start(out[bass.ds(j, 1)].rearrange("o p b t -> (o p) b t"), x3[:]).then_inc(stored, 16)

            def stack(i, _):
                if isinstance(i, int) and i == 0:
                    sp.wait_ge(setup_pool, 2)
                wait(sp, act_kh, i + 1)
                save(x1_hi, k_parts, 0, k_saved)
                save(x1_hi, k_parts, 2, k_saved)
                wait(sp, act_proj, 5 * i + 4)
                save(s2_hi, q_parts, 0, q_saved)
                save(s2_hi, q_parts, 1, q_saved)
                wait(sp, dve_q, 2 * i + 1)
                save(s2_lo, q_parts, 2, q_saved)
                wait(sp, dve_k_lo, i + 1)
                save(x1_lo, k_parts, 1, k_saved)
                wait(sp, q_saved, SAVES * (i + 1))
                stack_rows(qstack, q_parts, q_stacked)
                wait(sp, k_saved, SAVES * (i + 1))
                pad_rows(k_parts, k_padded)
                stack_rows(kstack, k_parts, k_stacked)

            def save(tile, parts, part, s):
                sp.dma_start(parts[:, part].rearrange("j d g b t -> j (d g) (b t)"),
                             flat(tile).bitcast(F32)).then_inc(s, 16)

            def stack_rows(tile, parts, s):
                sp.dma_start(tile[0:STACKED].bitcast(F32),
                             parts.rearrange("j s d g b t -> (j s d) g b t")).then_inc(s, 16)

            def pad_rows(parts, s):
                for jj in range(J):
                    row = PARTS * DH * jj
                    sp.dma_start(padded[row:row + PARTS * DH, :, :, jj, :].bitcast(F32),
                                 parts[jj].rearrange("s d g b t -> (s d) g b t")).then_inc(s, 16)

            def mq(i, _):
                wait(sp, pe_s, 16 * (i + 1))
                pad_rows(q_parts, q_padded)
                wait(sp, dve_mt, i + 1)
                for jj in range(J):
                    row = STACKED + DH * jj
                    sp.dma_start(padded[row:row + 1, :, :, jj, :].bitcast(F32),
                                 mt[DH * jj:P:J * DH].bitcast(F32)).then_inc(m_stacked, 16)

            run({"consts": constants, "stage": stage, "split_w": split_w, "load": load, "load_s": load_s,
                 "f1": refill, "stack": stack, "mq": mq, "mix3": mix3, "last_mix3": mix3}, sp)
            sp.wait_ge(stored, 16 * groups)


        @block.gpsimd
        def _(pool):
            nc.gpsimd.memset(padded[:].bitcast(F32), 0.0).then_inc(setup_pool, 1)
            nc.gpsimd.memset(vpad[:], 0.0).then_inc(setup_pool, 1)
            pool.wait_ge(setup_pool, 2)

            def stack(i, _):
                wait(pool, act_proj, 5 * i + 5)
                pad(i, 0)
                pad(i, 1)

            def E(i, k):
                if k in (G, 2 * G):
                    pad(i, k // G + 1)

            def pad(i, b):
                wait(pool, dve_pre, i + 1)
                wait(pool, pe_av, 16 * i + 4 * (b - 1))
                v = v_sb[:, b].rearrange("p (h d) -> p h d", h=H)
                half = H // 2
                for t in range(2):
                    mask = mask_g[:, b:b + 1].unsqueeze(2).broadcast_to([P, half, DH])
                    nc.gpsimd.tensor_tensor(diagonal(vpad, b % 2, half * t, 64 * t),
                                            v[:, half * t:half * t + half], mask, ALU.mult)
                    last = nc.gpsimd.tensor_copy(diagonal(vpad, b % 2, half * t, 64 * (1 - t)), mask)
                last.then_inc(pool_vpad, 1)

            def diagonal(tile, buf, h0, c0):
                ap = tile[:, buf, h0:h0 + H // 2, c0:c0 + DH].copy()
                dims = [list(d) for d in ap.ap]
                dims[1][0] = dims[1][0] + DH
                return bass.AP(tensor=ap.tensor, offset=ap.offset, ap=dims)

            def self_sub(i, _):
                wait(pool, dve_mt, i + 1)
                wait(pool, dve_k_lo, i + 1)
                nc.gpsimd.tensor_tensor(kf[:], s_self[:], mt[:].bitcast(F32), ALU.subtract).then_inc(pool_sub, 1)

            def self_w(i, _):
                wait(pool, act_ps, i + 1)
                wait(pool, act_proj, 5 * i + 3)
                nc.gpsimd.tensor_tensor(v_self[:], v_self[:], kf[:], ALU.mult).then_inc(pool_pv, 1)

            def fin(i, pair):
                two = slice(2 * pair, 2 * pair + 2)
                wait(pool, act_fin, 8 * i + 4 * pair + 2)
                nc.gpsimd.tensor_tensor(k_self[:, two], k_self[:, two], kf[:, two], ALU.add).then_inc(pool_den, 1)
                wait(pool, act_fin, 8 * i + 4 * pair + 4)
                wait(pool, pool_pv, i + 1)
                nc.gpsimd.tensor_tensor(s_self[:, two], s_self[:, two], v_self[:, two],
                                        ALU.add).then_inc(pool_num, 1)

            def att(i, pair):
                two = slice(2 * pair, 2 * pair + 2)
                wait(pool, dve_rec, 4 * i + 2 * (pair + 1))
                wait(pool, pool_num, 2 * i + pair + 1)
                nc.gpsimd.tensor_tensor(kf[:, two], s_self[:, two], k_self[:, two], ALU.mult).then_inc(pool_att, 1)

            def split2(j, _):
                wait(pool, act_x2, j + 1)
                nc.gpsimd.tensor_tensor(x2_lo[:], x2[:], x2_hi[:].bitcast(F32),
                                        ALU.subtract).then_inc(pool_x2_lo, 1)

            def exmix(j, _):
                wait(pool, act_out, NO * j + 5)
                wait(pool, dve_mix2, j + 1)
                one, two = outs[:, TILE[3]], outs[:, TILE[4]]
                nc.gpsimd.tensor_tensor(one, one, per_key(wab_g[:, 0]), ALU.mult).then_inc(pool_exmix, 1)
                nc.gpsimd.tensor_tensor(two, two, per_key(wab_g[:, 1]), ALU.mult).then_inc(pool_exmix, 1)
                wait(pool, pool_exmix, 3 * j + 2)
                nc.gpsimd.tensor_tensor(one, one, two, ALU.add).then_inc(pool_exmix, 1)

            def mix3(j, n):
                if n == 0:
                    wait(pool, dve_gate, 8 * (j + 1))
                term = outs[:, MIX3[ADD3[n]]]
                nc.gpsimd.tensor_tensor(term, term, per_key(gate[:, ADD3[n]]), ALU.mult).then_inc(pool_term, 1)
                wait(pool, pool_term, 4 * j + n + 1)
                if n:
                    wait(pool, mixed3, 4 * j + n)
                nc.gpsimd.tensor_tensor(x3[:], x3[:], term, ALU.add).then_inc(mixed3, 1)

            run({"stack": stack, "E": E, "self_sub": self_sub, "self_w": self_w, "fin": fin, "att": att,
                 "split2": split2,
                 "exmix": exmix, "mix3": mix3}, pool)

        def hi_passes(out_ap, a_hi, a_lo, b_hi, start=True):
            nc.tensor.matmul(out_ap, a_hi, b_hi, start=start, stop=False)
            nc.tensor.matmul(out_ap, a_lo, b_hi, start=False, stop=False)

        def lo_pass(out_ap, a_hi, b_lo, stop=True):
            return nc.tensor.matmul(out_ap, a_hi, b_lo, start=False, stop=stop)

        @block.tensor
        def _(pe):
            pe.wait_ge(consts_in, 16 * len(CONSTS))

            def biases(i, _):
                for k, (w, v) in enumerate(((0, 5), (1, 4), (1, 5), (3, 2))):
                    last = nc.tensor.matmul(bank_a[0][:, k:k + 1], wraw[:, w], vec[:, v:v + 1],
                                            start=True, stop=True)
                last.then_inc(setup_pe, 1)

            def lora1(i, _):
                wait(pe, x_in, 16 * (i + 1))
                wait(pe, act_fin, 8 * i)
                nc.tensor.matmul(bank_a[2][0:LR], lora_a[:], flat(x0), start=True, stop=True).then_inc(pe_lora, 1)

            def lora2(i, _):
                wait(pe, dve_adapt, 2 * (i + 1))
                nc.tensor.matmul(bank_a[3][:], lora_be[:], flat(adapt), start=True, stop=True).then_inc(pe_lora, 1)

            def proj(i, _):
                if isinstance(i, int) and i == 0:
                    pe.wait_ge(setup_act, 2)
                    pe.wait_ge(setup_dve, 1)
                wait(pe, act_x1, i + 1)
                hi_passes(bank_a[3][:], w_hi[:, 1], w_lo[:, 1], flat(x1_hi))
                wait(pe, dve_x1_lo, i + 1)
                lo_pass(bank_a[3][:], w_hi[:, 1], flat(x1_lo)).then_inc(pe_proj, 1)
                wait(pe, act_s2, i + 1)
                wait(pe, dve_x2, i)
                wait(pe, act_exp, 16 * i)
                wait(pe, dve_s2_lo, i + 1)
                for bank, w in ((0, 1), (1, 2), (2, 0)):
                    hi_passes(bank_a[bank][:], w_hi[:, w], w_lo[:, w], flat(s2_hi))
                    lo_pass(bank_a[bank][:], w_hi[:, w], flat(s2_lo)).then_inc(pe_proj, 1)
                wait(pe, act_proj, 5 * i + 3)
                for b in range(NB):
                    last = nc.tensor.matmul(bank_a[1][:, b * P:b * P + P], x1[:, b], wraw[:, 2],
                                            start=True, stop=True)
                last.then_inc(pe_proj, 1)

            def self_(i, _):
                wait(pe, dve_q, 2 * i + 2)
                nc.tensor.matmul(bank_a[0][:], head_sum, flat(k_self), start=True, stop=True).then_inc(pe_self, 1)

            def S(i, n):
                b, g = divmod(n, G)
                if n == 0:
                    wait(pe, q_stacked, STACKS * (i + 1))
                    wait(pe, k_padded, PADS * (i + 1))
                    wait(pe, act_self, i + 1)
                    wait(pe, act_proj, 5 * i + 5)
                if n >= 2:
                    wait(pe, dve_max, 16 * i + n - 1)
                nc.tensor.matmul(bank_a[n % 2][:], qstack[:, g, b],
                                 padded[0:STACKED, g, b].rearrange("p j t -> p (j t)"),
                                 start=True, stop=True).then_inc(pe_s, 1)
                if b and g == G - 1:
                    turn_max(i, b - 1)

            def turn_max(i, b):
                wait(pe, act_mexp, NB * i + b + 1)
                last = nc.tensor.transpose(bank_a[2][:, b * P:b * P + P],
                                           m_exp[:, b % 2].rearrange("p h d -> p (h d)"), ident)
                last.then_inc(pe_mt, 1)

            def mq(i, _):
                turn_max(i, NB - 1)

            def av(i, k):
                b, g = divmod(k, G)
                wait(pe, act_exp, 16 * i + k + 1)
                if g == 0:
                    wait(pe, pool_vpad, NB * i + b + 1)
                    if b == 0:
                        wait(pe, dve_mt, i + 1)
                for jj in range(J):
                    h = J * g + jj
                    half, hh = divmod(h, H // 2)
                    last = nc.tensor.matmul(attended(b, half), vpad[:, b % 2, h],
                                            probs[:, k % 2, jj], start=(hh == 0), stop=(hh == H // 2 - 1))
                last.then_inc(pe_av, 1)

            def E(i, k):
                b, g = divmod(k, G)
                if isinstance(i, int) and i == 0 and k == 0:
                    pe.wait_ge(setup_act, 3)
                if k == 0:
                    wait(pe, k_stacked, STACKS * (i + 1))
                    wait(pe, q_padded, PADS * (i + 1))
                    wait(pe, m_stacked, PADS * (i + 1))
                    wait(pe, dve_max, 16 * (i + 1))
                if k >= 2:
                    wait(pe, act_exp, 16 * i + k - 1)
                nc.tensor.matmul(bank_a[k % 2][:], kstack[:, g, b],
                                 padded[:, g, b].rearrange("p j t -> p (j t)"),
                                 start=True, stop=True).then_inc(pe_st, 1)
                if k:
                    av(i, k - 1)

            def Eend(i, _):
                av(i, NB * G - 1)

            def wo(i, _):
                wait(pe, pool_att, 2 * (i + 1))
                nc.tensor.matmul(bank_a[0][:], wraw[:, 3], flat(kf), start=True, stop=True).then_inc(pe_wo, 1)

            def f1(j, u):
                o, c = divmod(u, 4)
                layer, kind, e = OUTS[o]
                if u == 0:
                    wait(pe, dve_x2, j + 1)
                if isinstance(j, int) and j == 0 and u == SHARED2_FIRST:
                    pe.wait_ge(setup_act, 3 + NS)
                    pe.wait_ge(setup_dve, 1 + NS)
                if u == SHARED2_FIRST:
                    wait(pe, act_x2, j + 1)
                if L3_FIRST <= u < L3_FIRST + NB:
                    wait(pe, dve_term, 12 * j + mixed(2, u - L3_FIRST))
                if u == SHARED3_FIRST:
                    wait(pe, act_x3, j + 1)
                wait(pe, act_unit, UNITS * j + u - 1)
                wait(pe, dve_lo, NSHARED * j + SHARED_BEFORE[u - 1] if u else NSHARED * j)
                bank = bank_h[u % 2]
                if kind == "shared":
                    w = slice(c * P, c * P + P)
                    hi_passes(bank[:], sh_hi[:, e, w], sh_lo[:, e, w], flat(x2_hi))
                    if u == SHARED2_FIRST:
                        wait(pe, pool_x2_lo, j + 1)
                    if u == SHARED3_FIRST:
                        wait(pe, dve_x3_lo, j + 1)
                    last = lo_pass(bank[:], sh_hi[:, e, w], flat(x2_lo))
                else:
                    n = EXPERT_UNITS.index(u)
                    loads = 2 if n % RING < NE - RING else 1
                    wait(pe, ring_in[n % RING], 16 * (loads * j + n // RING + 1))
                    src = (x2 if layer == 2 else x3)[:, c]
                    for cc in range(FC):
                        last = nc.tensor.matmul(bank[:, cc * P:cc * P + P], ring[:, n % RING, cc * P:cc * P + P],
                                                src, start=True, stop=True)
                last.then_inc(pe_f1, 1)

            free_o = [(act_out, NO, 0), (dve_logit, 2, 0), (act_out, NO, 1), (act_out, NO, 3),
                      (dve_logit, 2, 1), (act_out, NO, 4), (act_out, NO, 5), (act_out, NO, 6)]

            def f2(j, u):
                o, c = divmod(u, 4)
                _, kind, e = OUTS[o]
                bank = bank_o[slot_o[o]]
                if c == 0:
                    s, per, n = free_o[o]
                    wait(pe, s, per * j + n)
                wait(pe, act_unit, UNITS * j + u + 1)
                if kind == "shared":
                    w = slice(F + c * P, F + c * P + P)
                    hi_passes(bank[:], sh_hi[:, e, w], sh_lo[:, e, w], h_hi[:, u % 2], start=(c == 0))
                    wait(pe, dve_lo, NSHARED * j + SHARED_BEFORE[u + 1])
                    last = lo_pass(bank[:], sh_hi[:, e, w], h_lo[:, u % 2], stop=(c == FC - 1))
                else:
                    n = EXPERT_UNITS.index(u)
                    for cc in range(FC):
                        last = nc.tensor.matmul(bank[:, c * P:c * P + P],
                                                ring[:, n % RING, F + cc * P:F + cc * P + P], h_ex[:, u % 2, cc],
                                                start=(cc == 0), stop=(cc == FC - 1))
                last.then_inc(pe_f2, 1)

            def hid_(j, layer):
                if isinstance(j, int) and j == 0 and layer == 0:
                    pe.wait_ge(late_in, 16 * len(LATE_CONSTS))
                if layer == 0:
                    wait(pe, act_out, NO * j + 3)
                    w, terms = g1_sb, MIX2
                else:
                    wait(pe, act_out, NO * j + 8)
                    wait(pe, pool_exmix, 3 * (j + 1))
                    w, terms = gw1_sb, MIX3
                for n, o in enumerate(terms):
                    last = nc.tensor.matmul(bank_o[1][:, 0:NB], w[:, n], outs[:, o, :, 0],
                                            start=(n == 0), stop=(n == len(terms) - 1))
                last.then_inc(pe_hid, 1)

            def logit(j, layer):
                wait(pe, dve_hid, 2 * j + layer + 1)
                n = 3 + layer
                nc.tensor.matmul(bank_o[1][:, 8:8 + NB * n], all_sum,
                                 weighed[:, 0:n].rearrange("p w b -> p (w b)"),
                                 start=True, stop=True).then_inc(pe_logit, 1)

            run({"biases": biases, "lora1": lora1, "lora2": lora2, "proj": proj, "self": self_, "S": S, "mq": mq, "E": E,
                 "Eend": Eend, "wo": wo, "f1": f1, "f2": f2, "hid": hid_,
                 "logit": logit}, pe)

        @block.scalar
        def _(act):
            def high(dst, src):
                return nc.scalar.activation(dst, src, ACT.Copy)

            act.wait_ge(consts_in, 16 * len(CONSTS))
            nc.scalar.activation(w_hi[:, 0], wraw[:, 0], ACT.Copy, scale=SCALE).then_inc(setup_act, 1)
            high(w_hi[:, 1:3], wraw[:, 1:3]).then_inc(setup_act, 1)

            def weights(i, _):
                nc.scalar.activation(kstack[STACKED:P].rearrange("p g b t -> p (g b t)"),
                                     shift_row[STACKED:P].broadcast_to([32, G * NB * P]), ACT.Copy).then_inc(setup_act, 1)
                act.wait_ge(setup_gate, 1)
                nc.scalar.activation(gv[:], gv[:], ACT.Exp).then_inc(setup_gate_exp, 1)

            def split_w(i, e):
                if e == 0:
                    act.wait_ge(stage_in, 16 * NS)
                high(sh_hi[:, e], ring[:, e]).then_inc(setup_act, 1)

            def split_s(i, _):
                wait(act, s_in, 16 * (i + 1))
                wait(act, q_saved, SAVES * i)
                high(s2_hi[:], s2[:]).then_inc(act_s2, 1)

            def lora2(i, _):
                wait(act, dve_x1, i + 1)
                wait(act, k_saved, SAVES * i)
                high(x1_hi[:], x1[:]).then_inc(act_x1, 1)

            def proj(i, _):
                if isinstance(i, int) and i == 0:
                    act.wait_ge(setup_dve, 1)
                wait(act, pool_att, 2 * i)
                wait(act, pe_wo, i)
                wait(act, pe_proj, 5 * i + 1)
                nc.scalar.activation(flat(kf), bank_a[3][:], ACT.Identity, bias=bias[:, 1:2]).then_inc(act_proj, 1)
                wait(act, pe_proj, 5 * i + 2)
                nc.scalar.activation(flat(k_self), bank_a[0][:], ACT.Identity, bias=bias[:, 2:3]).then_inc(act_proj, 1)
                wait(act, pe_proj, 5 * i + 3)
                nc.scalar.activation(flat(v_self), bank_a[1][:], ACT.Copy).then_inc(act_proj, 1)
                wait(act, pe_proj, 5 * i + 4)
                wait(act, dve_s2_lo, i + 1)
                nc.scalar.activation(flat(s2_hi), bank_a[2][:], ACT.Identity, bias=bias[:, 0:1]).then_inc(act_proj, 1)
                wait(act, dve_kf, i + 1)
                wait(act, dve_x1_lo, i + 1)
                high(x1_hi[:], kf[:]).then_inc(act_kh, 1)
                wait(act, pe_proj, 5 * i + 5)
                wait(act, pool_vpad, NB * i)
                nc.scalar.activation(flat(v_sb), bank_a[1][:], ACT.Copy).then_inc(act_proj, 1)

            def self_(i, _):
                wait(act, pe_self, i + 1)
                wait(act, dve_s2_lo, i + 1)
                nc.scalar.activation(flat(s_self), bank_a[0][:], ACT.Copy).then_inc(act_self, 1)

            def E(i, k):
                wait(act, pe_st, 16 * i + k + 1)
                if k >= 2:
                    wait(act, pe_av, 16 * i + k - 1)
                nc.scalar.activation(probs[:, k % 2].rearrange("p j t -> p (j t)"), bank_a[k % 2][:],
                                     ACT.Exp).then_inc(act_exp, 1)

            def mexp(i, b):
                wait(act, dve_max, 16 * i + G * (b + 1))
                if b >= 2:
                    wait(act, pe_mt, NB * i + b - 1)
                nc.scalar.activation(m_exp[:, b % 2], m_nat[:, b].unsqueeze(2).broadcast_to([P, H, DH]),
                                     ACT.Copy).then_inc(act_mexp, 1)

            def self_w(i, _):
                wait(act, pool_sub, i + 1)
                nc.scalar.activation(kf[:], kf[:], ACT.Exp).then_inc(act_ps, 1)

            def fin(i, pair):
                wait(act, pe_av, 16 * i + 8 * (pair + 1))
                lo, hi = slice(0, 64), slice(64, P)
                two = slice(2 * pair, 2 * pair + 2)
                sums = bank_a[2 + pair][:].rearrange("p (b h t) -> p b h t", b=2, h=2)
                for dst, rows_out, rows_in, half in ((k_self, lo, hi, 0), (k_self, hi, lo, 1),
                                                     (s_self, lo, lo, 0), (s_self, hi, hi, 1)):
                    nc.scalar.activation(dst[rows_out, two], sums[rows_in, :, half], ACT.Copy).then_inc(act_fin, 1)

            def split2(i, _):
                wait(act, dve_x2, i + 1)
                wait(act, pe_f1, UNITS * i)
                high(x2_hi[:], x2[:]).then_inc(act_x2, 1)

            def f1(j, u):
                wait(act, pe_f1, UNITS * j + u + 1)
                if u >= 2:
                    wait(act, pe_f2, UNITS * j + u - 1)
                elif not (isinstance(j, int) and j == 0):
                    wait(act, pe_f2, UNITS * j)
                kind = OUTS[u // 4][1]
                dst = h_hi[:, u % 2] if kind == "shared" else h_ex[:, u % 2].rearrange("p c t -> p (c t)")
                nc.scalar.activation(dst, bank_h[u % 2][:], ACT.Relu).then_inc(act_unit, 1)


            def f2(j, u):
                o, c = divmod(u, 4)
                if c < 3:
                    return
                wait(act, pe_f2, UNITS * j + u + 1)
                if o == 0:
                    wait(act, pool_exmix, 3 * j)
                if o == 1 and not (isinstance(j, int) and j == 0):
                    wait(act, mixed3, 4 * j - 3)
                if o == 4:
                    wait(act, dve_mix2, j + 1)
                nc.scalar.activation(outs[:, TILE[o]].rearrange("p b t -> p (b t)"), bank_o[slot_o[o]][:],
                                     ACT.Copy).then_inc(act_out, 1)

            def soft(j, layer):
                wait(act, dve_logit, 2 * j + layer + 1)
                n = 3 + layer
                nc.scalar.activation(gate[:, 0:n], gate[:, 0:n], ACT.Exp).then_inc(act_gate, 1)

            def split3(j, _):
                wait(act, dve_mix2, j + 1)
                wait(act, pe_f1, UNITS * j + L3_FIRST)
                high(x2_hi[:], x3[:]).then_inc(act_x3, 1)

            run({"weights": weights, "split_w": split_w, "lora2": lora2, "split_s": split_s, "proj": proj,
                 "self": self_, "mexp": mexp, "self_w": self_w, "E": E, "fin": fin, "split2": split2,
                 "f1": f1, "f2": f2, "soft": soft, "split3": split3}, act)

        @block.vector
        def _(dve):
            def low(dst, src, hi):
                return nc.vector.tensor_tensor(dst, src, hi.bitcast(F32), ALU.subtract)

            class Chain:
                def __init__(self, s):
                    self.s, self.n, self.base = s, 0, 0

                def __call__(self, ins):
                    ins.then_inc(self.s, 1)
                    self.n += 1

                def settle(self):
                    dve.wait_ge(self.s, self.base + self.n)

            c = Chain(setup_chain)
            dve.wait_ge(consts_in, 16 * len(CONSTS))
            c(nc.vector.tensor_copy(lens_f[:], ints[:, 0]))
            c(nc.vector.tensor_copy(labels_f[:], ints[:, 1]))
            c(nc.vector.tensor_copy(langs_f[:], ints[:, 2]))
            c.settle()
            c(nc.vector.tensor_scalar(key_mask[:], lens_f[:], part_no, None, ALU.is_gt))
            c(nc.vector.tensor_scalar(lang_hot[:], langs_f[:], lang_no, None, ALU.is_equal))
            c.settle()

            def biases(i, _):
                dve.wait_ge(setup_act, 2)
                nc.vector.scalar_tensor_tensor(w_lo[:, 0], wraw[:, 0], SCALE, w_hi[:, 0].bitcast(F32), ALU.mult,
                                               ALU.subtract)
                low(w_lo[:, 1:3], wraw[:, 1:3], w_hi[:, 1:3])
                dve.wait_ge(setup_pe, 1)
                c(nc.vector.tensor_scalar(bias[:, 0:1], bank_a[0][:, 0:1], vec[:, 0:1], SCALE, ALU.add, ALU.mult))
                c(nc.vector.tensor_scalar(bias[:, 1:3], bank_a[0][:, 1:3], vec[:, 1:2], None, ALU.add))
                c(nc.vector.tensor_scalar(bias[:, 3:4], bank_a[0][:, 3:4], vec[:, 3:4], None, ALU.add))
                c.settle()
                nc.vector.tensor_copy(bq_s[:], bias[:, 0:1]).then_inc(setup_dve, 1)

            def weights(i, _):
                dve.wait_ge(late_in, 16 * len(LATE_CONSTS))
                c(nc.vector.tensor_reduce(gv_s[:], gv[:], AXX, ALU.max))
                c.settle()
                c(nc.vector.tensor_tensor(gv[:], gv[:], gv_s[:].unsqueeze(2).broadcast_to([P, TYPES, 4]), ALU.subtract))
                c.settle()
                nc.vector.tensor_scalar(gv[:], gv[:], 10.0, None, ALU.mult).then_inc(setup_gate, 1)
                dve.wait_ge(setup_gate_exp, 1)
                c(nc.vector.tensor_reduce(gv_s[:], gv[:], AXX, ALU.add))
                c.settle()
                c(nc.vector.reciprocal(gv_s[:], gv_s[:]))
                c.settle()
                c(nc.vector.tensor_tensor(gv[:], gv[:], gv_s[:].unsqueeze(2).broadcast_to([P, TYPES, 4]), ALU.mult))
                c.settle()
                for k in range(2):
                    c(nc.vector.tensor_scalar(wab[:, k], labels_f[:], 0.0, gv[:, 0, k:k + 1], ALU.is_equal, ALU.mult))
                    for t in range(1, TYPES):
                        c(nc.vector.tensor_scalar(wab_t, labels_f[:], float(t), gv[:, t, t + k:t + k + 1],
                                                  ALU.is_equal, ALU.mult))
                        c.settle()
                        c(nc.vector.tensor_tensor(wab[:, k], wab[:, k], wab_t, ALU.add))
                        c.settle()

            def split_w(i, e):
                dve.wait_ge(setup_act, 4 + e)
                low(sh_lo[:, e], ring[:, e], sh_hi[:, e]).then_inc(setup_dve, 1)

            def lora1(i, _):
                at = bass.ds(i * NB, NB)
                wait(dve, pe_lora, 2 * i)
                nc.vector.tensor_copy(hot_g[:], lang_hot[:, at]).then_inc(dve_tables, 1)
                nc.vector.tensor_copy(len_g[:], lens_f[:, at]).then_inc(dve_tables, 1)
                dve.wait_ge(dve_tables, 4 * i + 2)
                nc.vector.tensor_tensor(pad_key[:], key_no.unsqueeze(1).broadcast_to([P, NB, P]),
                                        per_key(len_g[:]), ALU.is_ge).then_inc(dve_tables, 1)
                nc.vector.tensor_copy(adapt[LR:LR + LANGS],
                                      per_key(hot_g[LR:LR + LANGS], LANGS)).then_inc(dve_adapt, 1)
                wait(dve, pe_lora, 2 * i + 1)
                nc.vector.tensor_tensor(adapt[0:LR], bank_a[2][0:LR].rearrange("p (b t) -> p b t", b=NB),
                                        per_key(hot_g[0:LR], LR), ALU.mult).then_inc(dve_adapt, 1)

            def split_s(i, _):
                wait(dve, act_s2, i + 1)
                wait(dve, q_saved, SAVES * i)
                low(s2_lo[:], s2[:], s2_hi[:]).then_inc(dve_s2_lo, 1)

            def lora2(i, _):
                wait(dve, dve_x2, i)
                wait(dve, pe_lora, 2 * i + 2)
                nc.vector.tensor_tensor(flat(x1), flat(x0), bank_a[3][:], ALU.add).then_inc(dve_x1, 1)
                wait(dve, act_x1, i + 1)
                wait(dve, k_saved, SAVES * i)
                low(x1_lo[:], x1[:], x1_hi[:]).then_inc(dve_x1_lo, 1)

            def proj(i, _):
                if isinstance(i, int) and i == 0:
                    dve.wait_ge(setup_dve, 1)
                wait(dve, act_proj, 5 * i + 1)
                nc.vector.tensor_copy(k_first[:], kf[:, :, 0]).then_inc(dve_tables, 1)
                dve.wait_ge(dve_tables, 4 * i + 4)
                wait(dve, pool_vpad, NB * i)
                nc.vector.tensor_copy(mask_g[:], key_mask[:, bass.ds(i * NB, NB)]).then_inc(dve_pre, 1)
                for b in range(NB):
                    last = nc.vector.copy_predicated(kf[:, b], pad_key[:, b], k_first[:, b:b + 1].broadcast_to([P, P]))
                last.then_inc(dve_kf, 1)
                wait(dve, act_proj, 5 * i + 4)
                nc.vector.scalar_tensor_tensor(flat(s2_lo), bank_a[2][:], bq_s[:, 0:1], flat(s2_hi).bitcast(F32),
                                               ALU.add, ALU.subtract).then_inc(dve_q, 1)
                wait(dve, act_kh, i + 1)
                low(x1_lo[:], kf[:], x1_hi[:]).then_inc(dve_k_lo, 1)
                nc.vector.scalar_tensor_tensor(flat(k_self), bank_a[2][:], bq_s[:, 0:1], flat(k_self),
                                               ALU.add, ALU.mult).then_inc(dve_q, 1)

            def S(i, n):
                b, g = divmod(n, G)
                wait(dve, pe_s, 16 * i + n + 1)
                nc.vector.tensor_reduce(m_nat[:, b, J * g:J * g + J],
                                        bank_a[n % 2][:].rearrange("p (j t) -> p j t", j=J),
                                        AXX, ALU.max).then_inc(dve_max, 1)

            def mq(i, _):
                wait(dve, pe_mt, NB * (i + 1))
                wait(dve, act_self, i + 1)
                wait(dve, m_stacked, PADS * i)
                nc.vector.tensor_tensor(flat(mt), bank_a[2][:], flat(s_self), ALU.max).then_inc(dve_mt, 1)

            def rec(i, b):
                wait(dve, pool_den, 2 * i + b // 2 + 1)
                nc.vector.reciprocal(k_self[:, b], k_self[:, b]).then_inc(dve_rec, 1)

            def wo(i, _):
                wait(dve, pe_wo, i + 1)
                if not (isinstance(i, int) and i == 0):
                    wait(dve, pe_f1, UNITS * (i - 1) + SHARED2_FIRST + 1)
                nc.vector.scalar_tensor_tensor(flat(x2), bank_a[0][:], bias[:, 3:4], flat(x1),
                                               ALU.add, ALU.add).then_inc(dve_x2, 1)

            def f1(j, u):
                if OUTS[u // 4][1] == "shared":
                    wait(dve, act_unit, UNITS * j + u + 1)
                    nc.vector.scalar_tensor_tensor(h_lo[:, u % 2], bank_h[u % 2][:], 0.0,
                                                   h_hi[:, u % 2].bitcast(F32), ALU.max,
                                                   ALU.subtract).then_inc(dve_lo, 1)

            def hid(j, layer):
                wait(dve, pe_hid, 2 * j + layer + 1)
                n = 3 + layer
                second = gw2_sb if layer else g2_sb
                nc.vector.scalar_tensor_tensor(weighed[:, 0:n],
                                               bank_o[1][:, 0:NB].unsqueeze(1).broadcast_to([P, n, NB]), 0.0,
                                               second[:].unsqueeze(2).broadcast_to([P, n, NB]), ALU.max,
                                               ALU.mult).then_inc(dve_hid, 1)

            def logit(j, layer):
                wait(dve, pe_logit, 2 * j + layer + 1)
                if layer == 0:
                    wait(dve, pool_term, 4 * j)
                n = 3 + layer
                lg = bank_o[1][:, 8:8 + NB * n].rearrange("p (w b) -> p w b", b=NB)
                nc.vector.tensor_reduce(gmax[:], lg.rearrange("p w b -> p b w"), AXX, ALU.max).then_inc(dve_gate, 1)
                dve.wait_ge(dve_gate, 8 * j + 4 * layer + 1)
                nc.vector.tensor_tensor(gate[:, 0:n], lg, gmax[:].unsqueeze(1).broadcast_to([P, n, NB]),
                                        ALU.subtract).then_inc(dve_logit, 1)

            def soft(j, layer):
                wait(dve, act_gate, 2 * j + layer + 1)
                n = 3 + layer
                base = 8 * j + 4 * layer
                nc.vector.tensor_reduce(gmax[:], gate[:, 0:n].rearrange("p w b -> p b w"), AXX,
                                        ALU.add).then_inc(dve_gate, 1)
                dve.wait_ge(dve_gate, base + 2)
                nc.vector.reciprocal(gmax[:], gmax[:]).then_inc(dve_gate, 1)
                dve.wait_ge(dve_gate, base + 3)
                nc.vector.tensor_tensor(gate[:, 0:n], gate[:, 0:n], gmax[:].unsqueeze(1).broadcast_to([P, n, NB]),
                                        ALU.mult).then_inc(dve_gate, 1)
                dve.wait_ge(dve_gate, base + 4)

            def mix2(j, _):
                wait(dve, stored, 16 * j)
                wait(dve, act_out, NO * j + 3)
                for pair in range(NB // 2):
                    for n in range(3):
                        for b in (2 * pair, 2 * pair + 1):
                            if n:
                                dve.wait_ge(dve_term, 12 * j + mixed(n - 1, b))
                            nc.vector.scalar_tensor_tensor(x3[:, b], outs[:, MIX2[n], b], gate[:, n, b:b + 1],
                                                           (x3 if n else x2)[:, b], ALU.mult,
                                                           ALU.add).then_inc(dve_term, 1)
                dve.wait_ge(dve_term, 12 * j + 12)
                nc.vector.tensor_copy(wab_g[:], wab[:, :, bass.ds(j * NB, NB)]).then_inc(dve_mix2, 1)

            def split3(j, _):
                wait(dve, act_x3, j + 1)
                low(x2_lo[:], x3[:], x2_hi[:]).then_inc(dve_x3_lo, 1)

            def last_mix3(j, n):
                if n == 0:
                    dve.wait_ge(pool_exmix, 3 * (j + 1))
                    dve.wait_ge(act_out, NO * (j + 1))
                    dve.wait_ge(pe_f1, UNITS * j + X3_EXPERTS)
                else:
                    dve.wait_ge(mixed3, 4 * j + n)
                for b in range(NB):
                    m = ADD3[n]
                    last = nc.vector.scalar_tensor_tensor(x3[:, b], outs[:, MIX3[m], b], gate[:, m, b:b + 1],
                                                          x3[:, b], ALU.mult, ALU.add)
                last.then_inc(mixed3, 1)

            run({"biases": biases, "lora1": lora1, "split_s": split_s, "lora2": lora2, "proj": proj, "S": S, "mq": mq,
                 "rec": rec, "wo": wo,
                 "f1": f1, "hid": hid, "logit": logit, "soft": soft, "mix2": mix2, "split3": split3, "last_mix3": last_mix3,
                 "weights": weights, "split_w": split_w}, dve)


def kernel(x, itok_B_0_3, fside_BxSxS_0, itok_B_18_1004, itok_B_0_2, L0_cond_lora_A, L0_cond_lora_B,
           L0_cond_lang_embed, L1_cond_Wq, L1_cond_bq, L1_cond_Wk, L1_cond_bk, L1_cond_Wv, L1_cond_bv,
           L1_cond_Wo, L1_cond_bo, L1_cond_b_prev, L1_cond_b_self, L2_cond_wi, L2_cond_wo, L2_cond_swi,
           L2_cond_swo, L2_cond_g1, L2_cond_g2, L3_cond_expert_wi, L3_cond_expert_wo, L3_cond_share_wi,
           L3_cond_share_wo, L3_cond_gate_vecs, L3_cond_gate_w1, L3_cond_gate_w2):
    import concourse.bacc as bacc
    from concourse.bass_utils import run_bass_kernel_spmd

    a = np.asarray
    B = a(x).shape[0]
    groups = B // NB

    def turned(t):
        return np.ascontiguousarray(a(t).reshape(groups, NB, P, P).transpose(0, 3, 1, 2))

    def rows(t):
        return np.ascontiguousarray(np.broadcast_to(a(t).reshape(1, -1), (P, a(t).size)))

    def expert(wi, wo):
        wi, wo = a(wi), a(wo)
        n = wi.shape[0]
        wo = wo.reshape(n, FC, P, P).transpose(0, 2, 1, 3).reshape(n, P, FC * P)
        return np.ascontiguousarray(np.concatenate([wi, wo], axis=2))

    def cut(w, n):
        return np.ascontiguousarray(a(w).reshape(n, P, P).transpose(1, 0, 2))

    p = np.arange(P)
    turn = p.reshape(G, J, DH).transpose(1, 2, 0).reshape(P)
    consts = np.zeros((P, 4 * P + 3), np.float32)
    consts[:, 0:P] = np.eye(P)
    consts[:, P:2 * P] = (turn[:, None] // DH == p[None, :] // DH)
    consts[:, 2 * P:3 * P] = p[None, :]
    consts[:, 3 * P:4 * P] = 1
    consts[:, 4 * P] = p
    consts[:, 4 * P + 1] = np.where(p < LR, p // RANK, p - LR)
    consts[:, 4 * P + 2] = np.where((p >= STACKED) & (p % DH == 0), -1, 0)

    shared = np.concatenate([expert(L2_cond_swi, L2_cond_swo), expert(L3_cond_share_wi, L3_cond_share_wo)])
    loraB = a(L0_cond_lora_B).transpose(0, 2, 1).reshape(LR, P)
    arrays = {
        "xT": turned(x), "sT": turned(fside_BxSxS_0),
        "lens": rows(itok_B_18_1004), "labels": rows(itok_B_0_2), "langs": rows(itok_B_0_3),
        "loraA": np.ascontiguousarray(a(L0_cond_lora_A).reshape(LR, P).T),
        "loraBe": np.concatenate([loraB, a(L0_cond_lang_embed)]),
        "wqkvo": np.ascontiguousarray(np.stack([a(L1_cond_Wq)[:, turn], a(L1_cond_Wk)[:, turn], a(L1_cond_Wv),
                                                a(L1_cond_Wo)], 1)),
        "vecs": np.ascontiguousarray(np.stack([a(v).reshape(P) for v in (
            a(L1_cond_bq)[turn], a(L1_cond_bk)[turn], L1_cond_bv, L1_cond_bo, L1_cond_b_prev, L1_cond_b_self)], 1)),
        "shared": np.ascontiguousarray(shared.transpose(1, 0, 2)),
        "experts2": expert(L2_cond_wi, L2_cond_wo), "experts3": expert(L3_cond_expert_wi, L3_cond_expert_wo),
        "g1": cut(L2_cond_g1, 3), "g2r": a(L2_cond_g2),
        "gw1": cut(L3_cond_gate_w1, 4), "gw2r": a(L3_cond_gate_w2),
        "gate_vecs": rows(L3_cond_gate_vecs).reshape(P, TYPES, 4),
        "consts": consts,
    }
    nc = bacc.Bacc("TRN2", target_bir_lowering=False, num_devices=1)
    args = [nc.dram_tensor(n, v.shape, mybir.dt.from_np(v.dtype), kind="ExternalInput").ap()
            for n, v in arrays.items()]
    out = nc.dram_tensor("out", (groups, P, NB, P), F32, kind="ExternalOutput").ap()
    parts = [nc.dram_tensor(n, s, F32, kind="Internal").ap()
             for n, s in (("q_parts", (J, PARTS, DH, G, NB, P)), ("k_parts", (J, PARTS, DH, G, NB, P)))]
    cond_resid_kernel(nc, *args, *parts, out)
    r = run_bass_kernel_spmd(nc, [arrays], core_ids=[0])
    got = r.results[0]["out"]
    return np.ascontiguousarray(np.asarray(got).transpose(0, 2, 3, 1).reshape(B, P, P))
```
